# Optimizing a Trainium2 kernel written in Bass

```python
import numpy as np
import jax
import jax.numpy as jnp

def _softmax(x, axis=-1):
    return jax.nn.softmax(x, axis=axis)
def _gelu(x):
    return jax.nn.gelu(x, approximate=True)
def _silu(x):
    return jax.nn.silu(x)
def _sigmoid(x):
    return jax.nn.sigmoid(x)
def _layernorm(x, axis=-1, eps=1e-5):
    m = jnp.mean(x, axis=axis, keepdims=True)
    v = jnp.var(x, axis=axis, keepdims=True)
    return (x - m) / jnp.sqrt(v + eps)
def _scatter_add(tgt, idx, src, axis=0):
    return tgt.at[idx].add(src)
def _segment_sum(src, seg, n):
    return jax.ops.segment_sum(src, seg, n)

kernel_name = 'mk_conv_seq_d1_conv_nhwc768_a1ea62'

def setup_inputs(seed: int = 0):
    np.random.seed(seed)
    _w = jnp.asarray
    def _rec_inputs():
        import jax
        import jax.numpy as jnp
        _gk = jax.random.key(seed)
        x = -0.0008768 + 1.001 * jax.random.normal(jax.random.fold_in(_gk, 1), (1, 48, 48, 768), jnp.float32)
        return x
    x = _rec_inputs()
    def _L0_conv_setup():
        import jax, jax.numpy as jnp
        import numpy as np
        NUM_HEADS = 12
        LN_EPS = 1e-05

        def layernorm(x, g, b):
            mu = jnp.mean(x, axis=-1, keepdims=True)
            var = jnp.var(x, axis=-1, keepdims=True)
            return (x - mu) * jax.lax.rsqrt(var + LN_EPS) * g + b

        def _block(x, qkv_w, qkv_b, proj_w, proj_b, rel_pos_h, rel_pos_w, ln1_g, ln1_b, ln2_g, ln2_b, mlp_w1, mlp_b1, mlp_w2, mlp_b2):
            B, H, W, C = x.shape
            nh = NUM_HEADS
            hd = C // nh
            scale = hd ** (-0.5)
            shortcut = x
            xn = layernorm(x, ln1_g, ln1_b)
            qkv = xn.reshape(B, H * W, C) @ qkv_w + qkv_b
            qkv = qkv.reshape(B, H * W, 3, nh, hd).transpose(2, 0, 3, 1, 4)
            qkv = qkv.reshape(3, B * nh, H * W, hd)
            q, k, v = (qkv[0], qkv[1], qkv[2])
            attn = jnp.einsum('bqc,bkc->bqk', q * scale, k)
            coords = jnp.arange(H)[:, None] - jnp.arange(H)[None, :] + (H - 1)
            Rh = rel_pos_h[coords]
            Rw = rel_pos_w[coords]
            r_q = q.reshape(B * nh, H, W, hd)
            rel_h = jnp.einsum('bhwc,hkc->bhwk', r_q, Rh)
            rel_w = jnp.einsum('bhwc,wkc->bhwk', r_q, Rw)
            attn = (attn.reshape(B * nh, H, W, H, W) + rel_h[:, :, :, :, None] + rel_w[:, :, :, None, :]).reshape(B * nh, H * W, H * W)
            attn = jax.nn.softmax(attn, axis=-1)
            out = jnp.einsum('bqk,bkc->bqc', attn, v)
            out = out.reshape(B, nh, H, W, hd).transpose(0, 2, 3, 1, 4).reshape(B, H, W, C)
            out = out @ proj_w + proj_b
            x = shortcut + out
            xn2 = layernorm(x, ln2_g, ln2_b)
            h = jax.nn.gelu(xn2 @ mlp_w1 + mlp_b1, approximate=False)
            return x + (h @ mlp_w2 + mlp_b2)
        key = jax.random.key(seed)
        ks = jax.random.split(key, 16)
        B, H, W, C = (1, 48, 48, 768)
        hd = C // NUM_HEADS
        mlp_dim = 4 * C
        L = 2 * H - 1
        s = 0.02
        return {'x': jax.random.normal(ks[0], (B, H, W, C), jnp.float32), 'qkv_w': jax.random.normal(ks[1], (C, 3 * C), jnp.float32) * s, 'qkv_b': jnp.zeros((3 * C,), jnp.float32), 'proj_w': jax.random.normal(ks[2], (C, C), jnp.float32) * s, 'proj_b': jnp.zeros((C,), jnp.float32), 'rel_pos_h': jax.random.normal(ks[3], (L, hd), jnp.float32) * s, 'rel_pos_w': jax.random.normal(ks[4], (L, hd), jnp.float32) * s, 'ln1_g': jnp.ones((C,), jnp.float32), 'ln1_b': jnp.zeros((C,), jnp.float32), 'ln2_g': jnp.ones((C,), jnp.float32), 'ln2_b': jnp.zeros((C,), jnp.float32), 'mlp_w1': jax.random.normal(ks[5], (C, mlp_dim), jnp.float32) * s, 'mlp_b1': jnp.zeros((mlp_dim,), jnp.float32), 'mlp_w2': jax.random.normal(ks[6], (mlp_dim, C), jnp.float32) * s, 'mlp_b2': jnp.zeros((C,), jnp.float32)}
    _L0_conv_all = _L0_conv_setup()
    _L0_conv_in = {k: v for k, v in _L0_conv_all.items() if k in ('qkv_w', 'qkv_b', 'proj_w', 'proj_b', 'rel_pos_h', 'rel_pos_w', 'ln1_g', 'ln1_b', 'ln2_g', 'ln2_b', 'mlp_w1', 'mlp_b1', 'mlp_w2', 'mlp_b2', )}
    del _L0_conv_all

    return {
        "x": x,
        "L0_conv_qkv_w": _L0_conv_in["qkv_w"],
        "L0_conv_qkv_b": _L0_conv_in["qkv_b"],
        "L0_conv_proj_w": _L0_conv_in["proj_w"],
        "L0_conv_proj_b": _L0_conv_in["proj_b"],
        "L0_conv_rel_pos_h": _L0_conv_in["rel_pos_h"],
        "L0_conv_rel_pos_w": _L0_conv_in["rel_pos_w"],
        "L0_conv_ln1_g": _L0_conv_in["ln1_g"],
        "L0_conv_ln1_b": _L0_conv_in["ln1_b"],
        "L0_conv_ln2_g": _L0_conv_in["ln2_g"],
        "L0_conv_ln2_b": _L0_conv_in["ln2_b"],
        "L0_conv_mlp_w1": _L0_conv_in["mlp_w1"],
        "L0_conv_mlp_b1": _L0_conv_in["mlp_b1"],
        "L0_conv_mlp_w2": _L0_conv_in["mlp_w2"],
        "L0_conv_mlp_b2": _L0_conv_in["mlp_b2"],
    }

def reference(x, L0_conv_qkv_w, L0_conv_qkv_b, L0_conv_proj_w, L0_conv_proj_b, L0_conv_rel_pos_h, L0_conv_rel_pos_w, L0_conv_ln1_g, L0_conv_ln1_b, L0_conv_ln2_g, L0_conv_ln2_b, L0_conv_mlp_w1, L0_conv_mlp_b1, L0_conv_mlp_w2, L0_conv_mlp_b2):
    import jax
    import jax.numpy as jnp
    def _L0_conv_ref(x, qkv_w, qkv_b, proj_w, proj_b, rel_pos_h, rel_pos_w, ln1_g, ln1_b, ln2_g, ln2_b, mlp_w1, mlp_b1, mlp_w2, mlp_b2):
        import jax, jax.numpy as jnp
        import numpy as np
        NUM_HEADS = 12
        LN_EPS = 1e-05

        def layernorm(x, g, b):
            mu = jnp.mean(x, axis=-1, keepdims=True)
            var = jnp.var(x, axis=-1, keepdims=True)
            return (x - mu) * jax.lax.rsqrt(var + LN_EPS) * g + b

        def _block(x, qkv_w, qkv_b, proj_w, proj_b, rel_pos_h, rel_pos_w, ln1_g, ln1_b, ln2_g, ln2_b, mlp_w1, mlp_b1, mlp_w2, mlp_b2):
            B, H, W, C = x.shape
            nh = NUM_HEADS
            hd = C // nh
            scale = hd ** (-0.5)
            shortcut = x
            xn = layernorm(x, ln1_g, ln1_b)
            qkv = xn.reshape(B, H * W, C) @ qkv_w + qkv_b
            qkv = qkv.reshape(B, H * W, 3, nh, hd).transpose(2, 0, 3, 1, 4)
            qkv = qkv.reshape(3, B * nh, H * W, hd)
            q, k, v = (qkv[0], qkv[1], qkv[2])
            attn = jnp.einsum('bqc,bkc->bqk', q * scale, k)
            coords = jnp.arange(H)[:, None] - jnp.arange(H)[None, :] + (H - 1)
            Rh = rel_pos_h[coords]
            Rw = rel_pos_w[coords]
            r_q = q.reshape(B * nh, H, W, hd)
            rel_h = jnp.einsum('bhwc,hkc->bhwk', r_q, Rh)
            rel_w = jnp.einsum('bhwc,wkc->bhwk', r_q, Rw)
            attn = (attn.reshape(B * nh, H, W, H, W) + rel_h[:, :, :, :, None] + rel_w[:, :, :, None, :]).reshape(B * nh, H * W, H * W)
            attn = jax.nn.softmax(attn, axis=-1)
            out = jnp.einsum('bqk,bkc->bqc', attn, v)
            out = out.reshape(B, nh, H, W, hd).transpose(0, 2, 3, 1, 4).reshape(B, H, W, C)
            out = out @ proj_w + proj_b
            x = shortcut + out
            xn2 = layernorm(x, ln2_g, ln2_b)
            h = jax.nn.gelu(xn2 @ mlp_w1 + mlp_b1, approximate=False)
            return x + (h @ mlp_w2 + mlp_b2)
        return _block(x, qkv_w, qkv_b, proj_w, proj_b, rel_pos_h, rel_pos_w, ln1_g, ln1_b, ln2_g, ln2_b, mlp_w1, mlp_b1, mlp_w2, mlp_b2)

    def _gn(v, G=32, eps=1e-5):
        B_, H_, W_, C_ = v.shape
        g = v.reshape(B_, H_, W_, G, C_ // G)
        m = jnp.mean(g, axis=(1, 2, 4), keepdims=True)
        s = jnp.var(g, axis=(1, 2, 4), keepdims=True)
        return ((g - m) / jnp.sqrt(s + eps)).reshape(v.shape)

    def _ln_c(v, eps=1e-6):
        m = jnp.mean(v, axis=-1, keepdims=True)
        s = jnp.var(v, axis=-1, keepdims=True)
        return (v - m) / jnp.sqrt(s + eps)

    def _ln_t(v, eps=1e-5):
        m = jnp.mean(v, axis=-1, keepdims=True)
        s = jnp.var(v, axis=-1, keepdims=True)
        return (v - m) / jnp.sqrt(s + eps)

    def _to_tokens(v):
        B_, H_, W_, C_ = v.shape
        return v.reshape(B_, H_ * W_, C_)
    def _from_tokens(t, like):
        return t.reshape(like.shape)

    x = _L0_conv_ref(x, L0_conv_qkv_w, L0_conv_qkv_b, L0_conv_proj_w, L0_conv_proj_b, L0_conv_rel_pos_h, L0_conv_rel_pos_w, L0_conv_ln1_g, L0_conv_ln1_b, L0_conv_ln2_g, L0_conv_ln2_b, L0_conv_mlp_w1, L0_conv_mlp_b1, L0_conv_mlp_w2, L0_conv_mlp_b2)
    return x


_drawn_inputs = setup_inputs


def setup_inputs(seed=0):
    import zlib

    import numpy as np

    out = dict(_drawn_inputs(seed))
    spreads = {'L0_conv_qkv_b': (0.0, 0.1),
     'L0_conv_proj_b': (0.0, 0.1),
     'L0_conv_ln1_g': (1.0, 0.6),
     'L0_conv_ln1_b': (0.0, 0.271),
     'L0_conv_ln2_g': (1.0, 0.2),
     'L0_conv_ln2_b': (0.0, 0.1),
     'L0_conv_mlp_b1': (0.0, 0.1),
     'L0_conv_mlp_b2': (0.0, 0.1)}
    factors = {'L0_conv_rel_pos_h': 8.0, 'L0_conv_rel_pos_w': 8.0}
    for name, (base, spread) in spreads.items():
        noise = np.random.default_rng([zlib.crc32(name.encode()), seed]).standard_normal(out[name].shape)
        drawn = base * np.exp(spread * noise) if base else spread * noise
        out[name] = jnp.asarray(drawn.astype(out[name].dtype))
    for name, factor in factors.items():
        out[name] = (out[name] * factor).astype(out[name].dtype)
    return out
```

```python
from contextlib import ExitStack

import concourse.bass as bass
from concourse import mybir

P = 128
GRID = 48
TOK = GRID * GRID
C = 768
NH = 12
HD = C // NH
F = 4 * C
KC = C // P
TT = TOK // P
CH = 384
NCH = TOK // CH
REL = 2 * GRID - 1
GW = 2 * REL
EPS = 1e-5
SCALE = float(HD) ** -0.5
LOWEST = -3.0e38
RING = 3

ALU = mybir.AluOpType
ACT = mybir.ActivationFunctionType
AX = mybir.AxisListType
F32 = mybir.dt.float32
F32R = mybir.dt.float32r
ds = bass.ds


def wait(eng, sem, value):
    if isinstance(value, int) and value <= 0:
        return
    eng.wait_ge(sem, value)


def passed(eng, count):
    eng.sem_inc(count, 1)


class Names:

    def __init__(self, nc, ctx):
        self.nc, self.ctx = nc, ctx

    def sb(self, name, shape, dt=F32):
        return self.ctx.enter_context(self.nc.sbuf_tensor(name, shape, dt))

    def ps(self, name, shape):
        return self.ctx.enter_context(self.nc.psum_tensor(name, shape, F32))

    def sem(self, name):
        return self.ctx.enter_context(self.nc.semaphore(name))


def statistics(v, x, stats, step):
    v.bn_stats(stats[:, 0:6], x[:, 0:CH]).then_inc(step, 1)
    v.bn_stats(stats[:, 6:12], x[:, CH:C]).then_inc(step, 1)


def inverse_variance(v, stats, mv, rvar, step, t):
    v.bn_aggr(mv[:, :], stats[:, :]).then_inc(step, 1)
    v.wait_ge(step, 5 * t + 3)
    v.tensor_scalar(rvar[:, :], mv[:, 1:2], EPS, None, ALU.add).then_inc(step, 1)
    v.wait_ge(step, 5 * t + 4)
    v.reciprocal(rvar[:, :], rvar[:, :]).then_inc(step, 1)


def normalise(v, out, x, mv, rstd):
    return v.tensor_scalar(out[:, :], x[:, :], mv[:, 0:1], rstd[:, 0:1], ALU.subtract, ALU.mult)


def phase_norm1(nc, io, con, scr, pp):
    with ExitStack() as ctx:
        n = Names(nc, ctx)
        x = [n.sb(f"n1_x{i}", [P, C]) for i in range(2)]
        xn = [n.sb(f"n1_xn{i}", [P, C]) for i in range(2)]
        y = [n.sb(f"n1_y{i}", [P, KC, P]) for i in range(2)]
        stats = [n.sb(f"n1_stats{i}", [P, 12]) for i in range(2)]
        mv = [n.sb(f"n1_mv{i}", [P, 2]) for i in range(2)]
        rvar = [n.sb(f"n1_rvar{i}", [P, 1]) for i in range(2)]
        rstd = [n.sb(f"n1_rstd{i}", [P, 1]) for i in range(2)]
        table = n.sb("n1_table", [P, 2 * REL])
        tp = [n.ps(f"n1_tp{i}", [P, 2, 512]) for i in range(2)]
        x_in = [n.sem(f"n1_x_in{i}") for i in range(2)]
        const_in, table_in = n.sem("n1_const_in"), n.sem("n1_table_in")
        var_step, root, normed = n.sem("n1_var_step"), n.sem("n1_root"), n.sem("n1_normed")
        xT_done, y_done, split = n.sem("n1_xT_done"), n.sem("n1_y_done"), n.sem("n1_split")
        zeroed, small = n.sem("n1_zeroed"), n.sem("n1_small")
        raw, w_hi, w_lo = pp["raw"], pp["w_hi"], pp["w_lo"]

        with nc.Block() as block:

            @block.sync
            def _(sp):
                for t in range(2):
                    sp.dma_start(x[t][:, :], io["x"][t * P:(t + 1) * P, :]).then_inc(x_in[t], 16)
                for dst, src in ((con["g1"], "ln1_g"), (con["b1n"], "ln1_b"), (con["g2"], "ln2_g"),
                                 (con["b2n"], "ln2_b"), (con["qk_b"], "qk_b"), (con["mlp_b1"], "mlp_b1")):
                    sp.dma_start(dst[:, :], io[src]).then_inc(const_in, 16)
                for dst, src in ((con["v_bias"], "v_b"), (con["proj_bias"], "proj_b"), (con["mlp_bias2"], "mlp_b2")):
                    sp.dma_start(dst[:, :], io[src].to_broadcast([P, C])).then_inc(const_in, 16)
                sp.dma_start(raw[:, :, :], io["w_qkv"][:, :, 0:CH]).then_inc(pp["raw_in"], 16)
                for half in range(2):
                    for j, src in enumerate(("rel_h", "rel_w")):
                        sp.dma_start(table[half * HD:(half + 1) * HD, j * REL:(j + 1) * REL],
                                     io[src]).then_inc(table_in, 16)
                with sp.Fori(1, TT // 2) as i:
                    for p in range(2):
                        t = 2 * i + p
                        sp.wait_ge(normed, t - 1)
                        sp.dma_start(x[p][:, :], io["x"][ds(t * P, P), :]).then_inc(x_in[p], 16)

            @block.gpsimd
            def _(pool):
                pool.memset(con["ident"][:, :], 0.0).then_inc(zeroed, 1)
                pool.wait_ge(zeroed, 1)
                pool.affine_select(out=con["ident"][:, :], in_=con["ident"][:, :], compare_op=ALU.not_equal, fill=1.0,
                                   base=0, pattern=[[-1, P]], channel_multiplier=1).then_inc(con["ident_done"], 1)

            @block.vector
            def _(v):
                def variance(t, p, between=lambda: None):
                    v.wait_ge(x_in[p], 16 * (t // 2) + 16)
                    statistics(v, x[p], stats[p], var_step)
                    v.wait_ge(var_step, 5 * t + 2)
                    between()
                    inverse_variance(v, stats[p], mv[p], rvar[p], var_step, t)

                def norm(t, p):
                    v.wait_ge(root, t + 1)
                    wait(v, xT_done, t - 1)
                    normalise(v, xn[p], x[p], mv[p], rstd[p]).then_inc(normed, 1)

                def split_tile(t, p):
                    v.wait_ge(y_done, t + 1)
                    hi = pp["xT_hi"][:, :, ds(t * P, P)]
                    v.tensor_copy(hi, y[p][:, :, :]).then_inc(split, 1)
                    v.wait_ge(split, 2 * t + 1)
                    v.tensor_tensor(pp["xT_lo"][:, :, ds(t * P, P)], y[p][:, :, :], hi.bitcast(F32),
                                    ALU.subtract).then_inc(split, 1)

                variance(0, 0)
                variance(1, 1)
                norm(0, 0)
                v.wait_ge(con["ident_done"], 1)
                v.tensor_tensor(con["fold"][:, :], con["ident"][:, 0:HD], con["ident"][:, HD:P],
                                ALU.add).then_inc(small, 1)
                v.wait_ge(const_in, 16 * 9)
                v.tensor_scalar(con["q_bias"][:, :], con["qk_b"][:, 0:KC], SCALE, None, ALU.mult).then_inc(small, 1)
                v.wait_ge(table_in, 64)
                v.tensor_scalar(table[:, :], table[:, :], 1.0 / SCALE, None, ALU.mult).then_inc(small, 1)
                v.wait_ge(small, 3)
                v.tensor_copy(con["rel_hi"][:, :], table[:, :]).then_inc(small, 1)
                v.wait_ge(small, 4)
                v.tensor_tensor(con["rel_lo"][:, :], table[:, :], con["rel_hi"][:, :].bitcast(F32),
                                ALU.subtract).then_inc(small, 1)
                v.wait_ge(pp["w_hi_done"], KC)
                v.tensor_tensor(w_lo[:, 0:KC * CH], raw[:, :, :].rearrange("p k c -> p (k c)"),
                                w_hi[:, 0:KC * CH].bitcast(F32), ALU.subtract).then_inc(pp["w_lo_done"], KC)
                with v.Fori(1, TT // 2) as i:
                    for p in range(2):
                        t = 2 * i + p
                        variance(t, p, lambda: norm(t - 1, 1 - p))
                        split_tile(t - 2, p)
                norm(TT - 1, 1)
                split_tile(TT - 2, 0)
                split_tile(TT - 1, 1)

            @block.tensor
            def _(pe):
                pe.wait_ge(con["ident_done"], 1)

                def turn(t, p):
                    pe.wait_ge(normed, t + 1)
                    wait(pe, y_done, t - 1)
                    for k in range(KC):
                        last = pe.transpose(tp[p][:, k // 3, (k % 3) * P:(k % 3 + 1) * P], xn[p][:, k * P:(k + 1) * P],
                                            con["ident"][:, :])
                    last.then_inc(xT_done, 1)

                turn(0, 0)
                turn(1, 1)
                with pe.Fori(1, TT // 2) as i:
                    for p in range(2):
                        turn(2 * i + p, p)

            @block.scalar
            def _(act):
                act.wait_ge(const_in, 16 * 9)

                def scale_shift(t, p):
                    act.wait_ge(xT_done, t + 1)
                    wait(act, split, 2 * t - 2)
                    for k in range(KC):
                        last = act.activation(y[p][:, k, :], tp[p][:, k // 3, (k % 3) * P:(k % 3 + 1) * P],
                                              ACT.Identity, scale=con["g1"][:, k:k + 1], bias=con["b1n"][:, k:k + 1])
                    last.then_inc(y_done, 1)

                def take_root(t, p):
                    act.wait_ge(var_step, 5 * t + 5)
                    act.activation(rstd[p][:, :], rvar[p][:, :], ACT.Sqrt).then_inc(root, 1)

                take_root(0, 0)
                take_root(1, 1)
                scale_shift(0, 0)
                act.wait_ge(pp["raw_in"], 16)
                act.activation(w_hi[:, 0:KC * CH], raw[:, :, :].rearrange("p k c -> p (k c)"),
                               ACT.Copy).then_inc(pp["w_hi_done"], KC)
                with act.Fori(1, TT // 2) as i:
                    for p in range(2):
                        t = 2 * i + p
                        take_root(t, p)
                        scale_shift(t - 1, 1 - p)
                scale_shift(TT - 1, 1)


def phase_qkv(nc, io, con, scr, pp):
    with ExitStack() as ctx:
        n = Names(nc, ctx)
        y = [n.sb(f"qk_y{i}", [P, CH]) for i in range(3)]
        slots = [n.sb(f"qkv_parts{i}", [P, 2 * CH], F32R) for i in range(3)]
        parts = [s[:, :].rearrange("p (a c) -> p a c", a=2) for s in slots]
        vparts = [s[:, :].rearrange("p (h a d) -> p h a d", a=2, d=HD) for s in slots]
        qst = [n.sb(f"rel_q{i}", [P, TOK], F32R) for i in range(2)]
        gs = [n.sb(f"rel_g{i}", [P, 2, GW]) for i in range(3)]
        ps = [n.ps(f"qkv_ps{i}", [P, 512]) for i in range(3)]
        gp = [n.ps(f"rel_ps{i}", [P, 512])[:, 0:2 * GW].rearrange("p (a c) -> p a c", a=2) for i in range(3)]
        raw, w_hi, w_lo, xT_hi, xT_lo = (pp[s] for s in ("raw", "w_hi", "w_lo", "xT_hi", "xT_lo"))
        raw_in, w_hi_done, w_lo_done = pp["raw_in"], pp["w_hi_done"], pp["w_lo_done"]
        mm, y_done, hi_done, lo_done = (n.sem(f"qk_{s}") for s in ("mm", "y_done", "hi_done", "lo_done"))
        out = [n.sem(f"qk_out{i}") for i in range(3)]
        q_in = [n.sem(f"rel_q_in{i}") for i in range(2)]
        q_all_out = n.sem("rel_q_all_out")
        g_mm, g_ev, rel_out = n.sem("rel_mm"), n.sem("rel_ev"), n.sem("rel_out")
        g_out = [n.sem(f"rel_g_out{i}") for i in range(3)]
        v_mm, v_y, v_hi, v_lo = (n.sem(f"v_{s}") for s in ("mm", "y", "hi", "lo"))
        v_out = [n.sem(f"v_out{i}") for i in range(3)]
        UNIT = KC * CH

        def rounds(eng, u, body):
            if u == 0:
                body(0)
            with eng.Fori(1 if u == 0 else 0, NCH) as ch:
                body(ch)

        with nc.Block() as block:

            @block.sync
            def _(sp):
                for s in range(3):
                    sp.sem_inc(g_out[s], 16)
                    sp.sem_inc(v_out[s], 16)
                sp.wait_ge(w_lo_done, KC)
                sp.dma_start(raw[:, :, :], io["w_qkv"][:, :, CH:2 * CH]).then_inc(raw_in, 16)
                for u in range(4):
                    def store(ch, u=u):
                        for oc in range(3):
                            sp.wait_ge(lo_done, 18 * u + 3 * ch + oc + 1)
                            row = (3 * (u % 2) + oc) * P
                            dst = scr["qk"][u // 2, :, row:row + P, ds(ch * CH, CH)].rearrange("a p t -> p a t")
                            sp.dma_start(dst, parts[oc][:, :, :].bitcast(F32)).then_inc(out[oc], 16)

                    rounds(sp, u, store)
                    if u == 1:
                        for s in range(3):
                            sp.wait_ge(out[s], 16 * 12)
                        sp.sem_inc(q_all_out, 1)
                    sp.wait_ge(w_lo_done, KC * (u + 2))
                    sp.dma_start(raw[:, :, :], io["w_qkv"][:, :, (u + 2) * CH:(u + 3) * CH]).then_inc(raw_in, 16)
                with sp.Fori(0, NH // 2) as i:
                    for p in range(2):
                        h = 2 * i + p
                        for j in range(TT // 2):
                            sp.wait_ge(g_ev, h * (TT // 2) + j + 1 + RING)
                            dst = scr["g"][h, 2 * j * P:(2 * j + 2) * P, :].rearrange("(a p) c -> p a c", p=P)
                            sp.dma_start(dst, gs[j % 3][:, :, :]).then_inc(g_out[j % 3], 16)
                        for s in range(3):
                            sp.wait_ge(g_out[s], 48 * h + 48 + 16)
                        base = h * TOK * GW
                        g = scr["g"]
                        rows = bass.AP(g.tensor, base + GRID - 1, [[GRID * GW - 1, GRID], [GW, GRID], [1, GRID]])
                        cols = bass.AP(g.tensor, base + REL + GRID - 1, [[GRID * GW, GRID], [GW - 1, GRID], [1, GRID]])
                        for j, src in enumerate((rows, cols)):
                            dst = scr["rel"][ds(h * TOK, TOK), j * GRID:(j + 1) * GRID].rearrange("(a b) c -> a b c", b=GRID)
                            sp.dma_start(dst, src).then_inc(rel_out, 16)
                with sp.Fori(0, 2) as half:
                    for t in range(TT):
                        sp.wait_ge(v_lo, TT * half + t + 1)
                        dst = scr["v"][t * P:(t + 1) * P, ds(half * (NH // 2), NH // 2), :, :]
                        sp.dma_start(dst, vparts[t % 3][:, :, :, :].bitcast(F32)).then_inc(v_out[t % 3], 16)
                for s in range(3):
                    sp.wait_ge(out[s], 16 * 24)
                    sp.wait_ge(v_out[s], 16 * 12 + 16)
                sp.wait_ge(rel_out, 32 * NH)

            @block.gpsimd
            def _(pool):
                pool.wait_ge(q_all_out, 1)

                def load(h, p):
                    wait(pool, g_mm, (TT // 2) * (h - 1))
                    for part in range(2):
                        pool.dma_start(qst[p][part * HD:(part + 1) * HD, :].bitcast(F32),
                                       scr["qk"][0, part, ds(h * HD, HD), :]).then_inc(q_in[p], 16)

                load(0, 0)
                load(1, 1)
                with pool.Fori(1, NH // 2) as i:
                    for p in range(2):
                        load(2 * i + p, p)

            @block.tensor
            def _(pe):
                for u in range(4):
                    pe.wait_ge(w_lo_done, KC * (u + 1))

                    def product(ch, u=u):
                        for oc in range(3):
                            wait(pe, y_done, 18 * u + 3 * ch + oc - 2)
                            for k in range(KC):
                                w0 = (u % 2) * UNIT + k * CH + oc * P
                                for q, (wt, xt) in enumerate(((w_hi, xT_hi), (w_hi, xT_lo), (w_lo, xT_hi))):
                                    last = pe.matmul(ps[oc][:, 0:CH], wt[:, w0:w0 + P], xt[:, k, ds(ch * CH, CH)],
                                                     start=(k == 0 and q == 0), stop=(k == KC - 1 and q == 2))
                            last.then_inc(mm, 1)

                    rounds(pe, u, product)
                with pe.Fori(0, NH // 2) as i:
                    for p in range(2):
                        h = 2 * i + p
                        pe.wait_ge(q_in[p], 32 * i + 32)
                        for j in range(TT // 2):
                            pe.wait_ge(g_ev, h * (TT // 2) + j + 1)
                            for a in range(2):
                                t = 2 * j + a
                                for q, tab in enumerate((con["rel_hi"], con["rel_lo"])):
                                    last = pe.matmul(gp[j % 3][:, a, 0:2 * REL], qst[p][:, t * P:(t + 1) * P],
                                                     tab[:, :], start=(q == 0), stop=(q == 1))
                            last.then_inc(g_mm, 1)
                pe.wait_ge(w_lo_done, KC * 6)
                with pe.Fori(0, 2) as half:
                    for t in range(TT):
                        pe.wait_ge(v_y, TT * half + t + 1)
                        for k in range(KC):
                            for q, (xt, wt) in enumerate(((xT_hi, w_hi), (xT_hi, w_lo), (xT_lo, w_hi))):
                                last = pe.matmul(ps[t % 3][:, 0:CH], xt[:, k, t * P:(t + 1) * P],
                                                 wt[:, ds(half * UNIT + k * CH, CH)],
                                                 start=(k == 0 and q == 0), stop=(k == KC - 1 and q == 2))
                        last.then_inc(v_mm, 1)

            @block.scalar
            def _(act):
                act.sem_inc(g_ev, RING)
                for u in range(4):
                    wait(act, mm, 18 * u)
                    act.wait_ge(raw_in, 16 * (u + 2))

                    def read_out(ch, u=u):
                        act.activation(w_hi[:, ds(((u + 1) % 2) * UNIT + ch * CH, CH)],
                                       raw[:, :, :].rearrange("p k c -> p (k c)")[:, ds(ch * CH, CH)],
                                       ACT.Copy).then_inc(w_hi_done, 1)
                        for oc in range(3):
                            tile = 18 * u + 3 * ch + oc
                            act.wait_ge(mm, tile + 1)
                            wait(act, lo_done, tile - 2)
                            if u < 2:
                                col = 3 * u + oc
                                bias, scale = con["q_bias"][:, col:col + 1], SCALE
                            else:
                                col = 3 * u + oc
                                bias, scale = con["qk_b"][:, col:col + 1], 1.0
                            act.activation(y[oc][:, :], ps[oc][:, 0:CH], ACT.Identity, scale=scale,
                                           bias=bias).then_inc(y_done, 1)

                    rounds(act, u, read_out)
                act.wait_ge(mm, 18 * 4)
                act.wait_ge(raw_in, 16 * 6)
                act.activation(w_hi[:, UNIT:2 * UNIT], raw[:, :, :].rearrange("p k c -> p (k c)"),
                               ACT.Copy).then_inc(w_hi_done, KC)
                with act.Fori(0, NH // 2) as i:
                    for p in range(2):
                        for j in range(TT // 2):
                            tile = (2 * i + p) * (TT // 2) + j
                            act.wait_ge(g_mm, tile + 1)
                            act.wait_ge(g_out[j % 3], 16 * (3 * (2 * i + p) + j // 3) + 16)
                            act.activation(gs[j % 3][:, :, :], gp[j % 3][:, :, :], ACT.Copy).then_inc(g_ev, 1)
                for s in range(3):
                    act.wait_ge(out[s], 16 * 24)
                with act.Fori(0, 2) as half:
                    for t in range(TT):
                        act.wait_ge(v_y, TT * half + t + 1 + RING)
                        act.wait_ge(v_out[t % 3], 16 * (6 * half + t // 3) + 16)
                        act.activation(vparts[t % 3][:, :, 0, :], y[t % 3][:, :].rearrange("p (h d) -> p h d", d=HD),
                                       ACT.Copy).then_inc(v_hi, 1)

            @block.vector
            def _(v):
                v.sem_inc(v_y, RING)
                for u in range(4):
                    def split(ch, u=u):
                        v.wait_ge(w_hi_done, KC * (u + 1) + ch + 1)
                        at = ds(((u + 1) % 2) * UNIT + ch * CH, CH)
                        v.tensor_tensor(w_lo[:, at], raw[:, :, :].rearrange("p k c -> p (k c)")[:, ds(ch * CH, CH)],
                                        w_hi[:, at].bitcast(F32), ALU.subtract).then_inc(w_lo_done, 1)
                        for oc in range(3):
                            tile = 18 * u + 3 * ch + oc
                            v.wait_ge(y_done, tile + 1)
                            wait(v, out[oc], 16 * (6 * u + ch))
                            v.tensor_copy(parts[oc][:, 0, :], y[oc][:, :]).then_inc(hi_done, 1)
                            v.wait_ge(hi_done, tile + 1)
                            v.tensor_tensor(parts[oc][:, 1, :], y[oc][:, :], parts[oc][:, 0, :].bitcast(F32),
                                            ALU.subtract).then_inc(lo_done, 1)

                    rounds(v, u, split)
                v.wait_ge(w_hi_done, KC * 6)
                v.tensor_tensor(w_lo[:, UNIT:2 * UNIT], raw[:, :, :].rearrange("p k c -> p (k c)"),
                                w_hi[:, UNIT:2 * UNIT].bitcast(F32), ALU.subtract).then_inc(w_lo_done, KC)
                with v.Fori(0, 2) as half:
                    for t in range(TT):
                        tile = TT * half + t
                        v.wait_ge(v_mm, tile + 1)
                        v.tensor_tensor(y[t % 3][:, :], ps[t % 3][:, 0:CH], con["v_bias"][:, ds(half * CH, CH)],
                                        ALU.add).then_inc(v_y, 1)
                        v.wait_ge(v_hi, tile + 1)
                        v.tensor_tensor(vparts[t % 3][:, :, 1, :], y[t % 3][:, :].rearrange("p (h d) -> p h d", d=HD),
                                        vparts[t % 3][:, :, 0, :].bitcast(F32), ALU.subtract).then_inc(v_lo, 1)


def phase_attention(nc, io, con, scr, nxt):
    KEYS = 2 * CH
    GROUPS = NH * NCH
    LOOP_FROM = 4
    with ExitStack() as ctx:
        n_ = Names(nc, ctx)
        keys = n_.sb("keys", [P, 2 * 2 * TOK], F32R)
        values = n_.sb("values", [P, TT, 2 * HD], F32R)
        qg = [n_.sb(f"queries{i}", [P, CH], F32R) for i in range(2)]
        relg = [n_.sb(f"rel{i}", [P, 3, 2 * GRID]) for i in range(2)]
        bias = [n_.sb(f"bias{i}", [P, KEYS]) for i in range(3)]
        probs = [n_.sb(f"probs{i}", [P, TOK]) for i in range(6)]
        pT_hi = [n_.sb(f"pT_hi{i}", [P, CH], F32R) for i in range(6)]
        pT_lo = [n_.sb(f"pT_lo{i}", [P, CH], F32R) for i in range(6)]
        mx = [n_.sb(f"max{i}", [P, 3]) for i in range(6)]
        nmax = [n_.sb(f"negmax{i}", [P, 1]) for i in range(6)]
        sums = [n_.sb(f"sums{i}", [P, 3, 3]) for i in range(2)]
        total = [n_.sb(f"total{i}", [P, 3]) for i in range(2)]
        rinv = [n_.sb(f"rinv{i}", [P, 3]) for i in range(2)]
        oT = [n_.sb(f"oT{i}", [P, CH]) for i in range(2)]
        o = [n_.sb(f"o{i}", [P, 3, HD]) for i in range(2)]
        w_raw = n_.sb("pr_w_raw", [P, KC * C])
        score_ps = [n_.ps(f"score_ps{i}", [P, 2, 512]) for i in range(2)]
        turn_ps = [n_.ps(f"turn_ps{i}", [P, 512]) for i in range(3)]
        out_ps = n_.ps("out_ps", [P, 512])

        q_in = [n_.sem(f"at_q_in{i}") for i in range(2)]
        rel_in = [n_.sem(f"at_rel_in{i}") for i in range(2)]
        k_in, sp_passed = n_.sem("at_k_in"), n_.sem("at_sp_passed")
        v_in = [n_.sem(f"at_v_in{i}") for i in range(3)]
        scored, added, biased = n_.sem("at_scored"), n_.sem("at_added"), n_.sem("at_biased")
        maxed, exped = n_.sem("at_maxed"), n_.sem("at_exped")
        turned, hi_done, lo_done = n_.sem("at_turned"), n_.sem("at_hi_done"), n_.sem("at_lo_done")
        multiplied, oT_done, folded = n_.sem("at_multiplied"), n_.sem("at_oT_done"), n_.sem("at_folded")
        inverted, normed = n_.sem("at_inverted"), n_.sem("at_normed")
        o_out = [n_.sem(f"at_o_out{i}") for i in range(2)]

        def groups(eng, step):
            def group(g, p):
                for s in range(9):
                    step(g, p, s)

            for g in range(LOOP_FROM):
                group(g, g % 2)
            with eng.Fori(LOOP_FROM // 2, GROUPS // 2) as i:
                for p in range(2):
                    group(2 * i + p, p)
            for g in range(GROUPS, GROUPS + 2):
                group(g, g % 2)

        def earlier(g, p, s, lag):
            back = -((s - lag) // 9)
            g2 = g - back
            if isinstance(g2, int) and not 0 <= g2 < GROUPS:
                return None
            return g2, (p + back) % 2, (s - lag) % 9

        def none(g):
            return isinstance(g, int) and not 0 <= g < GROUPS

        with nc.Block() as block:

            @block.sync
            def _(sp):
                def load_group(g, gi, h):
                    if isinstance(g, int) and g >= GROUPS:
                        return
                    p = gi % 2
                    wait(sp, scored, 9 * (g - 1))
                    wait(sp, biased, 9 * (g - 1))
                    passed(sp, sp_passed)
                    for part in range(2):
                        sp.dma_start(qg[p][part * HD:(part + 1) * HD, :].bitcast(F32),
                                     scr["qk"][0, part, ds(h * HD, HD), gi * CH:(gi + 1) * CH]).then_inc(q_in[p], 16)
                    sp.dma_start(relg[p][:, :, :], scr["rel"][ds(g * CH, CH), :].rearrange("(a p) c -> p a c", p=P))\
                        .then_inc(rel_in[p], 16)

                def load_keys(h):
                    wait(sp, scored, 9 * NCH * (h - 1))
                    passed(sp, sp_passed)
                    slot = (h % 2) * 2 * TOK
                    for dup in range(2):
                        for part in range(2):
                            sp.dma_start(keys[dup * HD:(dup + 1) * HD, ds(slot + part * TOK, TOK)].bitcast(F32),
                                         scr["qk"][1, part, ds(h * HD, HD), :]).then_inc(k_in, 16)

                def load_values(h, j):
                    wait(sp, multiplied, TT * (NCH * h - 1) + 6 * (j + 1) if not isinstance(h, int) or h else 0)
                    passed(sp, sp_passed)
                    src = scr["v"][j * 6 * P:(j + 1) * 6 * P, ds(h, 1), :, :].rearrange("(t p) h a d -> p (t h) (a d)", p=P)
                    sp.dma_start(values[:, j * 6:(j + 1) * 6, :].bitcast(F32), src).then_inc(v_in[j], 16)

                def store(g, gi, h):
                    if none(g):
                        return
                    sp.wait_ge(normed, g + 1)
                    passed(sp, sp_passed)
                    dst = scr["o"][gi * CH:(gi + 1) * CH, ds(h * HD, HD)].rearrange("(a p) c -> p a c", p=P)
                    sp.dma_start(dst, o[gi % 2][:, :, :]).then_inc(o_out[gi % 2], 16)

                def head(h, more=True):
                    for gi in range(NCH):
                        g = NCH * h + gi
                        if not (isinstance(g, int) and g == 0):
                            load_group(g + 1, (gi + 1) % NCH, h + (gi + 1) // NCH)
                        store(g - 2, (gi - 2) % NCH, h + (gi - 2) // NCH)
                        later = not (isinstance(h, int) and h == 0)
                        if gi == 0 and later:
                            load_values(h, 0)
                            load_values(h, 1)
                        if gi == 1 and later:
                            load_values(h, 2)
                        if gi == 1 and more:
                            load_keys(h + 1)

                load_group(0, 0, 0)
                load_keys(0)
                load_group(1, 1, 0)
                for j in range(3):
                    load_values(0, j)
                sp.dma_start(w_raw[:, :], io["w_proj"].rearrange("p k c -> p (k c)"))\
                    .then_inc(nxt["w_in"], 16)
                head(0)
                with sp.Fori(1, NH - 1) as h:
                    head(h)
                head(NH - 1, more=False)
                for gi in range(2):
                    store(GROUPS + gi - 2, NCH + gi - 2, NH - 1)
                for s in range(2):
                    sp.wait_ge(o_out[s], 16 * GROUPS // 2)

            @block.gpsimd
            def _(pool):
                def step(g, p, s):
                    if none(g):
                        return
                    n, qt, c = 9 * g + s, s // 3, s % 3
                    if s == 0:
                        pool.wait_ge(rel_in[p], 16 * (g // 2) + 16)
                    wait(pool, added, n - 2)
                    rows = relg[p][:, qt, c * 16:(c + 1) * 16].unsqueeze(2).to_broadcast([P, 16, GRID])
                    cols = relg[p][:, qt, GRID:2 * GRID].unsqueeze(1).to_broadcast([P, 16, GRID])
                    pool.tensor_tensor(bias[c][:, :].rearrange("p (a b) -> p a b", b=GRID), rows, cols,
                                       ALU.add).then_inc(biased, 1)

                groups(pool, step)

            @block.tensor
            def _(pe):
                def step(g, p, s):
                    n, qt, c = 9 * g + s, s // 3, s % 3
                    bank = score_ps[(p + s) % 2]
                    if s == 0 and not none(g):
                        pe.wait_ge(q_in[p], 32 * (g // 2) + 32)
                        pe.wait_ge(k_in, 64 * (g // NCH) + 64)
                    if not none(g):
                        wait(pe, added, n - 1)
                    if s == 5 and not none(g - 2):
                        pe.wait_ge(normed, g - 1)
                    if s == 3 and not none(g - 2):
                        pe.wait_ge(oT_done, g - 1)
                        if none(g):
                            wait(pe, added, 9 * GROUPS)
                        for t in range(3):
                            last = pe.matmul(bank[:, t // 2, CH + HD * (t % 2):CH + HD * (t % 2 + 1)],
                                             oT[p][:, t * P:(t + 1) * P], con["fold"][:, :], start=True, stop=True)
                        last.then_inc(folded, 1)
                    if not none(g):
                        slot = ((g // NCH) % 2) * 2 * TOK
                        for part in range(2):
                            for j in range(2):
                                last = pe.matmul(bank[:, j, 0:CH], qg[p][:, qt * P:(qt + 1) * P],
                                                 keys[:, ds(slot + (part * TOK + c * KEYS + j * CH), CH)],
                                                 start=(part == 0), stop=(part == 1))
                        last.then_inc(scored, 1)
                    turn = earlier(g, p, s, 10)
                    if turn:
                        g2, p2, u = turn
                        if u % 3 == 0:
                            pe.wait_ge(exped, 9 * g2 + 6 + u // 3 + 1)
                        for kt in (2 * u, 2 * u + 1):
                            wait(pe, lo_done, TT * g2 + kt - 2)
                            for t in range(3):
                                last = pe.transpose(turn_ps[kt % 3][:, t * P:(t + 1) * P],
                                                    probs[3 * p2 + t][:, kt * P:(kt + 1) * P], con["ident"][:, :])
                            last.then_inc(turned, 1)
                    product = earlier(g, p, s, 11)
                    if product:
                        g2, p2, u = product
                        if u % 3 == 0:
                            pe.wait_ge(v_in[u // 3], 16 * (g2 // NCH) + 16)
                        if u == 0:
                            wait(pe, oT_done, g2)
                        for kt in (2 * u, 2 * u + 1):
                            pe.wait_ge(lo_done, TT * g2 + kt + 1)
                            for q, part in enumerate((pT_hi, pT_lo)):
                                last = pe.matmul(out_ps[:, 0:CH], values[:, kt, :], part[kt % 6][:, :],
                                                 start=(kt == 0 and q == 0), stop=(kt == TT - 1 and q == 1))
                            last.then_inc(multiplied, 1)

                groups(pe, step)

            @block.vector
            def _(v):
                def score_waits(g, p, s):
                    if none(g):
                        return
                    n, c = 9 * g + s, s % 3
                    wait(v, turned, TT * (g - 2) + 6 * (c + 1) if not none(g - 2) else 0)
                    v.wait_ge(scored, n + 1)
                    v.wait_ge(biased, n + 1)

                def step(g, p, s):
                    n, qt, c = 9 * g + s, s // 3, s % 3
                    bank = score_ps[(p + s) % 2]
                    tile = 3 * p + qt
                    turn = earlier(g, p, s, 10)
                    if turn:
                        g2, p2, u = turn
                        for kt in (2 * u, 2 * u + 1):
                            v.wait_ge(hi_done, TT * g2 + kt + 1)
                            if kt % 2:
                                score_waits(g, p, s)
                            v.tensor_tensor(pT_lo[kt % 6][:, :], turn_ps[kt % 3][:, 0:CH],
                                            pT_hi[kt % 6][:, :].bitcast(F32), ALU.subtract).then_inc(lo_done, 1)
                    else:
                        score_waits(g, p, s)
                    if not none(g):
                        v.tensor_tensor_reduce(
                            out=probs[tile][:, c * KEYS:(c + 1) * KEYS].rearrange("p (a b) -> p a b", b=CH),
                            in0=bank[:, :, 0:CH], in1=bias[c][:, :].rearrange("p (a b) -> p a b", b=CH),
                            scale=1.0, scalar=LOWEST, op0=ALU.add, op1=ALU.max,
                            accum_out=mx[tile][:, c:c + 1]).then_inc(added, 1)
                        if c == 2:
                            v.wait_ge(added, n + 1)
                            v.tensor_reduce(nmax[tile][:, :], mx[tile][:, :], axis=AX.X, op=ALU.max,
                                            negate=True).then_inc(maxed, 1)
                    if s == 3 and not none(g - 2):
                        v.wait_ge(folded, g - 1)
                        v.wait_ge(inverted, 2 * g - 2)
                        if not none(g - 4):
                            v.wait_ge(o_out[p], 16 * ((g - 2) // 2))
                        for t in range(3):
                            last = v.tensor_scalar(o[p][:, t, :], bank[:, t // 2, CH + HD * (t % 2):CH + HD * (t % 2 + 1)],
                                                   rinv[p][:, t:t + 1], None, ALU.mult)
                        last.then_inc(normed, 1)
                    if s == 4 and not none(g - 1):
                        v.wait_ge(exped, 9 * g)
                        v.tensor_reduce(total[1 - p][:, :], sums[1 - p][:, :, :], axis=AX.X,
                                        op=ALU.add).then_inc(inverted, 1)
                        v.wait_ge(inverted, 2 * g - 1)
                        v.reciprocal(rinv[1 - p][:, :], total[1 - p][:, :]).then_inc(inverted, 1)
                    if isinstance(g, int) and g == GROUPS and s >= 3:
                        at = slice((s - 3) * C, (s - 2) * C)
                        v.wait_ge(nxt["w_split"], s - 2)
                        v.tensor_tensor(nxt["w_lo"][:, at], w_raw[:, at],
                                        nxt["w_hi"][:, at].bitcast(F32), ALU.subtract).then_inc(nxt["w_lo_done"], 1)

                groups(v, step)

            @block.scalar
            def _(act):
                def step(g, p, s):
                    if s == 2 and not none(g - 2):
                        act.wait_ge(multiplied, TT * (g - 1))
                        wait(act, folded, g - 3)
                        act.activation(oT[p][:, :], out_ps[:, 0:CH], ACT.Copy).then_inc(oT_done, 1)
                    turn = earlier(g, p, s, 10)
                    if turn:
                        g2, p2, u = turn
                        for kt in (2 * u, 2 * u + 1):
                            act.wait_ge(turned, TT * g2 + kt + 1)
                            wait(act, multiplied, TT * g2 + kt - 5)
                            act.activation(pT_hi[kt % 6][:, :], turn_ps[kt % 3][:, 0:CH], ACT.Copy).then_inc(hi_done, 1)
                    exp = earlier(g, p, s, 3)
                    if exp:
                        g2, p2, s2 = exp
                        qt, c = s2 // 3, s2 % 3
                        tile = 3 * p2 + qt
                        act.wait_ge(maxed, 3 * g2 + qt + 1)
                        at = probs[tile][:, c * KEYS:(c + 1) * KEYS]
                        act.activation(at, at, ACT.Exp, bias=nmax[tile][:, 0:1],
                                       accum_out=sums[p2][:, qt, c:c + 1]).then_inc(exped, 1)
                    if isinstance(g, int) and g == GROUPS and s >= 3:
                        act.wait_ge(nxt["w_in"], 16)
                        at = slice((s - 3) * C, (s - 2) * C)
                        act.activation(nxt["w_hi"][:, at], w_raw[:, at],
                                       ACT.Copy).then_inc(nxt["w_split"], 1)

                groups(act, step)


def phase_proj(nc, io, con, scr, nxt, mlp):
    with ExitStack() as ctx:
        n = Names(nc, ctx)
        w_hi, w_lo = nxt["w_hi"], nxt["w_lo"]
        o = [n.sb(f"pr_o{i}", [P, C]) for i in range(2)]
        x = [n.sb(f"pr_x{i}", [P, C]) for i in range(2)]
        oT_hi = [n.sb(f"pr_oT_hi{i}", [P, KC * P], F32R) for i in range(2)]
        oT_lo = [n.sb(f"pr_oT_lo{i}", [P, KC * P], F32R) for i in range(2)]
        x2 = [n.sb(f"pr_x2{i}", [P, C]) for i in range(2)]
        acc = [n.sb(f"pr_acc{i}", [P, C]) for i in range(2)]
        xn = [n.sb(f"pr_xn{i}", [P, C]) for i in range(2)]
        y = [n.sb(f"pr_y{i}", [P, KC, P]) for i in range(2)]
        parts = [n.sb(f"pr_parts{i}", [P, 2, KC, P], F32R) for i in range(2)]
        stats = [n.sb(f"pr_stats{i}", [P, 12]) for i in range(2)]
        mv = [n.sb(f"pr_mv{i}", [P, 2]) for i in range(2)]
        rvar = [n.sb(f"pr_rvar{i}", [P, 1]) for i in range(2)]
        rstd = [n.sb(f"pr_rstd{i}", [P, 1]) for i in range(2)]
        o_ps = n.ps("pr_o_ps", [P, 2, 512])
        mm_ps = n.ps("pr_mm_ps", [P, 2, 512])
        x_ps = n.ps("pr_x_ps", [P, 2, 512])
        sp_passed = n.sem("pr_sp_passed")
        o_in = [n.sem(f"pr_o_in{i}") for i in range(2)]
        x_in = [n.sem(f"pr_x_in{i}") for i in range(2)]
        oT_done, oT_hi_done, oT_lo_done = n.sem("pr_oT_done"), n.sem("pr_oT_hi_done"), n.sem("pr_oT_lo_done")
        xb_done, mm, x2_done, acc_done = n.sem("pr_xb_done"), n.sem("pr_mm"), n.sem("pr_x2_done"), n.sem("pr_acc_done")
        var_step, root, normed = n.sem("pr_var_step"), n.sem("pr_root"), n.sem("pr_normed")
        xT_done, y_done, split = n.sem("pr_xT_done"), n.sem("pr_y_done"), n.sem("pr_split")
        acc_out = [n.sem(f"pr_acc_out{i}") for i in range(2)]
        parts_out = [n.sem(f"pr_parts_out{i}") for i in range(2)]

        def tiles(eng, step):
            for t in range(4):
                step(t, t % 2)
            with eng.Fori(2, TT // 2 - 1) as i:
                for p in range(2):
                    step(2 * i + p, p)
            for t in range(TT - 2, TT):
                step(t, t % 2)

        with nc.Block() as block:

            @block.sync
            def _(sp):
                def load_o(t, p):
                    wait(sp, oT_done, t - 1)
                    passed(sp, sp_passed)
                    sp.dma_start(o[p][:, :], scr["o"][ds(t * P, P), :]).then_inc(o_in[p], 16)

                def load_x(t, p):
                    wait(sp, x2_done, t - 1)
                    passed(sp, sp_passed)
                    sp.dma_start(x[p][:, :], io["x"][ds(t * P, P), :]).then_inc(x_in[p], 16)

                def store(t, p):
                    sp.wait_ge(split, 2 * t + 2)
                    passed(sp, sp_passed)
                    sp.dma_start(scr["xT"][:, :, :, ds(t * P, P)], parts[p][:, :, :, :].bitcast(F32))\
                        .then_inc(parts_out[p], 16)

                def step(t, p):
                    more = not (isinstance(t, int) and t + 2 >= TT)
                    if more:
                        load_o(t + 2, p)
                    if not (isinstance(t, int) and t < 2):
                        store(t - 2, p)
                    if more:
                        load_x(t + 2, p)
                    if isinstance(t, int) and t == TT - 2:
                        for s in range(2):
                            sp.wait_ge(parts_out[s], 32)
                        for part in range(2):
                            sp.dma_start(mlp["xT0"][:, part, :, :].bitcast(F32),
                                         scr["xT"][:, part, :, 0:CH]).then_inc(mlp["first_x_in"], 16)

                for t in range(2):
                    load_o(t, t)
                    load_x(t, t)
                sp.dma_start(mlp["raw"][0][:, :].rearrange("p (k c) -> p k c", c=CH),
                             io["w_up"][:, :, 0:CH]).then_inc(mlp["raw_in"][0], 16)
                sp.dma_start(mlp["raw"][1][:, :].rearrange("p (f c) -> p f c", c=C),
                             io["w_down"][0:CH, :].rearrange("(f p) c -> p f c", p=P)).then_inc(mlp["raw_in"][1], 16)
                tiles(sp, step)
                store(TT - 2, 0)
                store(TT - 1, 1)
                for s in range(2):
                    sp.wait_ge(parts_out[s], 16 * TT // 2)
                    sp.wait_ge(acc_out[s], 16 * TT // 2)

            @block.gpsimd
            def _(pool):
                def add_bias(t, p):
                    pool.wait_ge(x_in[p], 16 * (t // 2) + 16)
                    pool.tensor_tensor(x[p][:, :], x[p][:, :], con["proj_bias"][:, :], ALU.add).then_inc(xb_done, 1)

                def step(t, p):
                    if not (isinstance(t, int) and t + 1 >= TT):
                        add_bias(t + 1, 1 - p)
                    pool.wait_ge(x2_done, t + 1)
                    if not (isinstance(t, int) and t < 2):
                        pool.wait_ge(acc_out[p], 16 * (t // 2))
                    pool.tensor_tensor(acc[p][:, :], x2[p][:, :], con["mlp_bias2"][:, :], ALU.add).then_inc(acc_done, 1)
                    pool.wait_ge(acc_done, t + 1)
                    pool.dma_start(scr["acc"][ds(t * P, P), :], acc[p][:, :]).then_inc(acc_out[p], 16)
                    if isinstance(t, int) and 1 <= t <= 3:
                        at = slice((t - 1) * C, t * C)
                        for i in range(2):
                            pool.wait_ge(mlp["split_hi"][i], t)
                            pool.tensor_tensor(mlp["w_lo"][i][0][:, at], mlp["raw"][i][:, at],
                                               mlp["w_hi"][i][0][:, at].bitcast(F32), ALU.subtract)\
                                .then_inc(mlp["split_lo"][i], 1)

                add_bias(0, 0)
                tiles(pool, step)

            @block.tensor
            def _(pe):
                def turn_o(t, p):
                    pe.wait_ge(o_in[p], 16 * (t // 2) + 16)
                    wait(pe, oT_lo_done, t)
                    for k in range(KC):
                        last = pe.transpose(o_ps[:, k // 3, (k % 3) * P:(k % 3 + 1) * P],
                                            o[p][:, k * P:(k + 1) * P], con["ident"][:, :])
                    last.then_inc(oT_done, 1)

                def turn_x(t, p):
                    pe.wait_ge(normed, t + 1)
                    wait(pe, y_done, t)
                    for k in range(KC):
                        last = pe.transpose(x_ps[:, k // 3, (k % 3) * P:(k % 3 + 1) * P],
                                            xn[p][:, k * P:(k + 1) * P], con["ident"][:, :])
                    last.then_inc(xT_done, 1)

                def step(t, p):
                    if not (isinstance(t, int) and t + 1 >= TT):
                        turn_o(t + 1, 1 - p)
                    pe.wait_ge(oT_lo_done, t + 1)
                    wait(pe, x2_done, t)
                    for nh in range(2):
                        for k in range(KC):
                            at = slice(k * P, (k + 1) * P)
                            to = slice(k * C + nh * CH, k * C + (nh + 1) * CH)
                            for q, (a, w) in enumerate(((oT_hi, w_hi), (oT_hi, w_lo), (oT_lo, w_hi))):
                                last = pe.matmul(mm_ps[:, nh, 0:CH], a[p][:, at], w[:, to],
                                                 start=(k == 0 and q == 0), stop=(k == KC - 1 and q == 2))
                    last.then_inc(mm, 1)
                    if not (isinstance(t, int) and t == 0):
                        turn_x(t - 1, 1 - p)

                turn_o(0, 0)
                pe.wait_ge(nxt["w_lo_done"], KC)
                tiles(pe, step)
                turn_x(TT - 1, 1)

            @block.scalar
            def _(act):
                def high(t, p):
                    act.wait_ge(oT_done, t + 1)
                    wait(act, mm, t - 1)
                    act.activation(oT_hi[p][:, :].rearrange("p (a b) -> p a b", b=CH), o_ps[:, :, 0:CH],
                                   ACT.Copy).then_inc(oT_hi_done, 1)

                def scale_shift(t, p):
                    act.wait_ge(xT_done, t + 1)
                    wait(act, split, 2 * t - 2)
                    for k in range(KC):
                        last = act.activation(y[p][:, k, :], x_ps[:, k // 3, (k % 3) * P:(k % 3 + 1) * P],
                                              ACT.Identity, scale=con["g2"][:, k:k + 1], bias=con["b2n"][:, k:k + 1])
                    last.then_inc(y_done, 1)

                def step(t, p):
                    if not (isinstance(t, int) and t + 1 >= TT):
                        high(t + 1, 1 - p)
                    if not (isinstance(t, int) and t == 0):
                        scale_shift(t - 1, 1 - p)
                    act.wait_ge(var_step, 5 * t + 5)
                    act.activation(rstd[p][:, :], rvar[p][:, :], ACT.Sqrt).then_inc(root, 1)
                    if isinstance(t, int) and 1 <= t <= 3:
                        at = slice((t - 1) * C, t * C)
                        for i in range(2):
                            act.wait_ge(mlp["raw_in"][i], 16)
                            act.activation(mlp["w_hi"][i][0][:, at], mlp["raw"][i][:, at],
                                           ACT.Copy).then_inc(mlp["split_hi"][i], 1)

                high(0, 0)
                tiles(act, step)
                scale_shift(TT - 1, 1)

            @block.vector
            def _(v):
                def low(t, p):
                    v.wait_ge(oT_hi_done, t + 1)
                    v.tensor_tensor(oT_lo[p][:, :].rearrange("p (a b) -> p a b", b=CH), o_ps[:, :, 0:CH],
                                    oT_hi[p][:, :].bitcast(F32).rearrange("p (a b) -> p a b", b=CH),
                                    ALU.subtract).then_inc(oT_lo_done, 1)

                def split_tile(t, p):
                    v.wait_ge(y_done, t + 1)
                    if not (isinstance(t, int) and t < 2):
                        v.wait_ge(parts_out[p], 16 * (t // 2))
                    v.tensor_copy(parts[p][:, 0, :, :], y[p][:, :, :]).then_inc(split, 1)
                    v.wait_ge(split, 2 * t + 1)
                    v.tensor_tensor(parts[p][:, 1, :, :], y[p][:, :, :], parts[p][:, 0, :, :].bitcast(F32),
                                    ALU.subtract).then_inc(split, 1)

                def step(t, p):
                    if not (isinstance(t, int) and t + 1 >= TT):
                        low(t + 1, 1 - p)
                    v.wait_ge(mm, t + 1)
                    v.wait_ge(xb_done, t + 1)
                    wait(v, acc_done, t - 1)
                    v.tensor_tensor(x2[p][:, :].rearrange("p (a b) -> p a b", b=CH), mm_ps[:, :, 0:CH],
                                    x[p][:, :].rearrange("p (a b) -> p a b", b=CH), ALU.add).then_inc(x2_done, 1)
                    v.wait_ge(x2_done, t + 1)
                    statistics(v, x2[p], stats[p], var_step)
                    v.wait_ge(var_step, 5 * t + 2)
                    if not (isinstance(t, int) and t == 0):
                        split_tile(t - 1, 1 - p)
                    inverse_variance(v, stats[p], mv[p], rvar[p], var_step, t)
                    v.wait_ge(root, t + 1)
                    wait(v, xT_done, t - 1)
                    normalise(v, xn[p], x2[p], mv[p], rstd[p]).then_inc(normed, 1)

                low(0, 0)
                tiles(v, step)
                split_tile(TT - 1, 1)


def phase_mlp(nc, io, con, scr, out, mlp):
    FG = F // CH
    UNITS = 2 * 3 * FG
    HT = TOK // 2
    with ExitStack() as ctx:
        n_ = Names(nc, ctx)

        def sem(name):
            return n_.sem(f"ml_{name}")

        xT = [mlp["xT0"]] + [n_.sb(f"ml_xT{i}", [P, 2, KC, CH], F32R) for i in (1, 2)]
        acc = n_.sb(f"ml_acc", [P, HT // P, C])
        raw = mlp["raw"]
        w_hi, w_lo = mlp["w_hi"], mlp["w_lo"]
        y = [n_.sb(f"ml_y{i}", [P, CH]) for i in range(3)]
        h_hi = [n_.sb(f"ml_h_hi{i}", [P, 3, CH], F32R) for i in range(2)]
        h_lo = [n_.sb(f"ml_h_lo{i}", [P, 3, CH], F32R) for i in range(2)]
        h_ps = [n_.ps(f"ml_h_ps{i}", [P, 512]) for i in range(3)]
        o_ps = [n_.ps(f"ml_o_ps{i}", [P, 512]) for i in range(3)]
        x_in = [sem(f"x_in{i}") for i in range(3)]
        acc_in, stored = [sem(f"acc_in{i}") for i in range(3)], [sem(f"stored{i}") for i in range(2)]
        raw_in, split_hi, split_lo = mlp["raw_in"], mlp["split_hi"], mlp["split_lo"]
        h_mm, gelu, hi_done, lo_done = sem("h_mm"), sem("gelu"), sem("h_hi"), sem("h_lo")
        o_mm, added = sem("o_mm"), sem("added")
        b1 = [n_.sb(f"ml_b1_{i}", [P, 3]) for i in range(2)]
        b1_done = sem("b1_done")

        def units(eng, step):
            for m in range(6):
                step(m, m)
            with eng.Fori(1, UNITS // 6 - 1) as i:
                for j in range(6):
                    step(6 * i + j, j)
            for m in range(UNITS - 6, UNITS):
                step(m, m % 6)

        def group_of(m, j):
            return (m - j) // 3 + j // 3 if not isinstance(m, int) else m // 3

        def last_group(m):
            return isinstance(m, int) and m // 3 == 2 * FG - 1

        def rows(dram, hf, tc):
            at = hf * HT + tc * CH
            return dram[at:at + CH, :].rearrange("(t p) c -> p t c", p=P)

        with nc.Block() as block:

            @block.sync
            def _(sp):
                def load_raw(i, fg):
                    wait(sp, split_lo[i], 3 * fg)
                    if i == 0:
                        src = io["w_up"][:, :, ds((fg % FG) * CH, CH)]
                        dst = raw[0][:, :].rearrange("p (k c) -> p k c", c=CH)
                    else:
                        src = io["w_down"][ds((fg % FG) * CH, CH), :].rearrange("(f p) c -> p f c", p=P)
                        dst = raw[1][:, :].rearrange("p (f c) -> p f c", c=C)
                    sp.dma_start(dst, src).then_inc(raw_in[i], 16)

                def step(m, j):
                    if j % 3 and not (isinstance(m, int) and m // 3 >= 2 * FG - 2):
                        load_raw(j % 3 - 1, group_of(m, j) + 2)

                load_raw(0, 1)
                load_raw(1, 1)
                units(sp, step)
                for tc in range(3):
                    sp.wait_ge(added, 6 * (UNITS - 2 + tc))
                    sp.dma_start(rows(out, 1, tc), acc[:, 3 * tc:3 * tc + 3, :]).then_inc(stored[1], 16)
                sp.wait_ge(stored[1], 16 * 3)

            @block.gpsimd
            def _(pool):
                def load_tokens(hf, tc):
                    at = hf * HT + tc * CH
                    for part in range(2):
                        pool.dma_start(xT[tc][:, part, :, :].bitcast(F32),
                                       scr["xT"][:, part, :, at:at + CH]).then_inc(x_in[tc], 16)

                def load_acc(hf, tc):
                    pool.dma_start(acc[:, 3 * tc:3 * tc + 3, :], rows(scr["acc"], hf, tc)).then_inc(acc_in[tc], 16)

                def copy_bias(fg):
                    wait(pool, gelu, 9 * (fg - 1))
                    at = 3 * (fg % FG)
                    pool.tensor_copy(b1[fg % 2][:, :], con["mlp_b1"][:, at:at + 3]).then_inc(b1_done, 1)

                copy_bias(0)
                load_tokens(0, 1)
                load_acc(0, 0)
                load_tokens(0, 2)
                load_acc(0, 1)
                load_acc(0, 2)
                for fg in range(1, FG + 1):
                    copy_bias(fg)
                for tc in range(3):
                    m = 3 * (FG - 1) + tc
                    pool.wait_ge(h_mm, 3 * m + 3)
                    load_tokens(1, tc)
                    pool.wait_ge(added, 6 * m + 6)
                    pool.dma_start(rows(out, 0, tc), acc[:, 3 * tc:3 * tc + 3, :]).then_inc(stored[0], 16)
                    pool.wait_ge(stored[0], 16 * (tc + 1))
                    load_acc(1, tc)
                for fg in range(FG + 1, 2 * FG):
                    copy_bias(fg)

            @block.tensor
            def _(pe):
                def hidden(m, j):
                    tc, slot = j % 3, (j // 3) % 2
                    if tc == 0:
                        pe.wait_ge(split_lo[0], 3 * group_of(m, j) + 3)
                    wait(pe, x_in[tc], 32 * (m // (3 * FG)) + (32 if tc else 0))
                    for f in range(3):
                        n = 3 * m + f
                        wait(pe, gelu, n - 2)
                        for k in range(KC):
                            w0 = k * CH + f * P
                            for q, (w, part) in enumerate(((w_hi, 0), (w_hi, 1), (w_lo, 0))):
                                last = pe.matmul(h_ps[f][:, 0:CH], w[0][slot][:, w0:w0 + P],
                                                 xT[tc][:, part, k, :],
                                                 start=(k == 0 and q == 0), stop=(k == KC - 1 and q == 2))
                        last.then_inc(h_mm, 1)

                def down(m, j):
                    tc, slot = j % 3, (j // 3) % 2
                    if tc == 0:
                        pe.wait_ge(split_lo[1], 3 * group_of(m, j) + 3)
                    pe.wait_ge(lo_done, 3 * m + 3)
                    for r in range(6):
                        tt, nh = r // 2, r % 2
                        wait(pe, added, 6 * m + r - 2)
                        for f in range(3):
                            to = slice(f * C + nh * CH, f * C + (nh + 1) * CH)
                            for q, (h, w) in enumerate(((h_hi, w_hi), (h_hi, w_lo), (h_lo, w_hi))):
                                last = pe.matmul(o_ps[r % 3][:, 0:CH], h[j % 2][:, f, tt * P:(tt + 1) * P],
                                                 w[1][slot][:, to], start=(f == 0 and q == 0), stop=(f == 2 and q == 2))
                        last.then_inc(o_mm, 1)

                def step(m, j):
                    hidden(m, j)
                    if not (isinstance(m, int) and m == 0):
                        down(m - 1, (j - 1) % 6)

                pe.wait_ge(mlp["first_x_in"], 32)
                units(pe, step)
                down(UNITS - 1, 5)

            @block.scalar
            def _(act):
                def split_piece(i, fg, slot, piece):
                    at = slice(piece * C, (piece + 1) * C)
                    act.activation(w_hi[i][slot][:, at], raw[i][:, at], ACT.Copy).then_inc(split_hi[i], 1)

                def step(m, j):
                    tc = j % 3
                    fg = group_of(m, j)
                    if tc and not last_group(m):
                        act.wait_ge(raw_in[tc - 1], 16 * (fg + 2))
                        wait(act, o_mm, 18 * fg)
                    if tc == 0:
                        act.wait_ge(b1_done, fg + 1)
                    for f in range(3):
                        if tc and not last_group(m):
                            split_piece(tc - 1, fg + 1, (j // 3 + 1) % 2, f)
                        n = 3 * m + f
                        wait(act, lo_done, n - 2)
                        act.wait_ge(h_mm, n + 1)
                        act.activation(y[f][:, :], h_ps[f][:, 0:CH], ACT.Gelu,
                                       bias=b1[(j // 3) % 2][:, f:f + 1]).then_inc(gelu, 1)

                units(act, step)

            @block.vector
            def _(v):
                def split_piece(i, fg, slot, piece):
                    at = slice(piece * C, (piece + 1) * C)
                    v.wait_ge(split_hi[i], 3 * fg + piece + 1)
                    v.tensor_tensor(w_lo[i][slot][:, at], raw[i][:, at], w_hi[i][slot][:, at].bitcast(F32),
                                    ALU.subtract).then_inc(split_lo[i], 1)

                def add_up(m, j):
                    tc = j % 3
                    v.wait_ge(acc_in[tc], 16 * (m // (3 * FG)) + 16)
                    for r in range(6):
                        tt, nh = r // 2, r % 2
                        q = 6 * m + r
                        v.wait_ge(o_mm, q + 1)
                        wait(v, added, q - 17)
                        at = acc[:, 3 * tc + tt, nh * CH:(nh + 1) * CH]
                        v.tensor_tensor(at, at, o_ps[r % 3][:, 0:CH], ALU.add).then_inc(added, 1)

                def step(m, j):
                    tc = j % 3
                    fg = group_of(m, j)
                    wait(v, o_mm, 6 * (m - 1))
                    for f in range(3):
                        if tc and not last_group(m):
                            split_piece(tc - 1, fg + 1, (j // 3 + 1) % 2, f)
                        n = 3 * m + f
                        v.wait_ge(gelu, n + 1)
                        v.tensor_copy(h_hi[j % 2][:, f, :], y[f][:, :]).then_inc(hi_done, 1)
                        v.wait_ge(hi_done, n + 1)
                        v.tensor_tensor(h_lo[j % 2][:, f, :], y[f][:, :], h_hi[j % 2][:, f, :].bitcast(F32),
                                        ALU.subtract).then_inc(lo_done, 1)
                    if not (isinstance(m, int) and m == 0):
                        add_up(m - 1, (j - 1) % 6)

                units(v, step)
                add_up(UNITS - 1, 5)


def build(nc, io, out):
    with ExitStack() as ctx:
        n = Names(nc, ctx)

        def dram(name, shape):
            return nc.dram_tensor(name, shape, F32, kind="Internal").ap()

        scr = {
            "qk": dram("qk_parts", (2, 2, C, TOK)),
            "v": dram("v_parts", (TOK, NH, 2, HD)),
            "g": dram("rel_products", (NH, TOK, GW)),
            "rel": dram("rel_terms", (NH * TOK, 2 * GRID)),
            "o": dram("attention_out", (TOK, C)),
            "acc": dram("x2_plus_b2", (TOK, C)),
            "xT": dram("norm2_parts", (P, 2, KC, TOK)),
        }
        con = {
            "ident": n.sb("ident", [P, P]), "fold": n.sb("fold", [P, HD]),
            "g1": n.sb("g1", [P, KC]), "b1n": n.sb("b1n", [P, KC]), "g2": n.sb("g2", [P, KC]), "b2n": n.sb("b2n", [P, KC]),
            "qk_b": n.sb("qk_b", [P, 2 * KC]), "q_bias": n.sb("q_bias", [P, KC]), "mlp_b1": n.sb("mlp_b1", [P, F // P]),
            "v_bias": n.sb("v_bias", [P, C]), "proj_bias": n.sb("proj_bias", [P, C]), "mlp_bias2": n.sb("mlp_bias2", [P, C]),
            "rel_hi": n.sb("rel_hi", [P, 2 * REL], F32R), "rel_lo": n.sb("rel_lo", [P, 2 * REL], F32R),
            "ident_done": n.sem("ident_done"),
        }
        with ExitStack() as inner:
            m = Names(nc, inner)
            pp = {
                "xT_hi": m.sb("xT_hi", [P, KC, TOK], F32R), "xT_lo": m.sb("xT_lo", [P, KC, TOK], F32R),
                "raw": m.sb("qkv_raw", [P, KC, CH]),
                "w_hi": m.sb("qkv_w_hi", [P, 2 * KC * CH], F32R), "w_lo": m.sb("qkv_w_lo", [P, 2 * KC * CH], F32R),
                "raw_in": m.sem("qkv_raw_in"), "w_hi_done": m.sem("qkv_w_hi_done"), "w_lo_done": m.sem("qkv_w_lo_done"),
            }
            phase_norm1(nc, io, con, scr, pp)
            phase_qkv(nc, io, con, scr, pp)
        with ExitStack() as rest:
            r = Names(nc, rest)
            mlp = {
                "first_x_in": r.sem("ml_first_x_in"),
                "raw_in": [r.sem(f"ml_raw_in{i}") for i in range(2)],
                "split_hi": [r.sem(f"ml_split_hi{i}") for i in range(2)],
                "split_lo": [r.sem(f"ml_split_lo{i}") for i in range(2)],
            }
            proj = {
                "w_hi": r.sb("pr_w_hi", [P, KC * C], F32R), "w_lo": r.sb("pr_w_lo", [P, KC * C], F32R),
                "w_in": r.sem("pr_w_in"), "w_split": r.sem("pr_w_split"), "w_lo_done": r.sem("pr_w_lo_done"),
            }
            phase_attention(nc, io, con, scr, proj)
            mlp["raw"] = [r.sb(f"ml_raw{i}", [P, KC * CH]) for i in range(2)]
            second = [slice(i * KC * CH, (i + 1) * KC * CH) for i in range(2)]
            mlp["w_hi"] = [[r.sb(f"ml_w{i}_hi", [P, KC * CH], F32R), proj["w_hi"][:, second[i]]] for i in range(2)]
            mlp["w_lo"] = [[r.sb(f"ml_w{i}_lo", [P, KC * CH], F32R), proj["w_lo"][:, second[i]]] for i in range(2)]
            mlp["xT0"] = r.sb("ml_xT0", [P, 2, KC, CH], F32R)
            phase_proj(nc, io, con, scr, proj, mlp)
            phase_mlp(nc, io, con, scr, out, mlp)


def kernel(x, L0_conv_qkv_w, L0_conv_qkv_b, L0_conv_proj_w, L0_conv_proj_b, L0_conv_rel_pos_h, L0_conv_rel_pos_w,
           L0_conv_ln1_g, L0_conv_ln1_b, L0_conv_ln2_g, L0_conv_ln2_b, L0_conv_mlp_w1, L0_conv_mlp_b1,
           L0_conv_mlp_w2, L0_conv_mlp_b2):
    import numpy as np
    import concourse.bacc as bacc
    from concourse.bass_utils import run_bass_kernel_spmd

    def tiled(w):
        w = np.asarray(w)
        return np.ascontiguousarray(w.reshape(-1, P, w.shape[1]).transpose(1, 0, 2))

    def columns(b):
        return np.ascontiguousarray(np.asarray(b).reshape(-1, P).T)

    def reversed_table(r):
        return np.ascontiguousarray(np.asarray(r)[::-1].T)

    qkv_b = np.asarray(L0_conv_qkv_b)
    arrays = {
        "x": np.ascontiguousarray(np.asarray(x).reshape(TOK, C)),
        "w_qkv": tiled(L0_conv_qkv_w), "w_proj": tiled(L0_conv_proj_w), "w_up": tiled(L0_conv_mlp_w1),
        "w_down": np.ascontiguousarray(L0_conv_mlp_w2),
        "qk_b": columns(qkv_b[:2 * C]), "v_b": qkv_b[None, 2 * C:].copy(),
        "proj_b": np.asarray(L0_conv_proj_b)[None, :].copy(), "mlp_b2": np.asarray(L0_conv_mlp_b2)[None, :].copy(),
        "mlp_b1": columns(L0_conv_mlp_b1),
        "ln1_g": columns(L0_conv_ln1_g), "ln1_b": columns(L0_conv_ln1_b),
        "ln2_g": columns(L0_conv_ln2_g), "ln2_b": columns(L0_conv_ln2_b),
        "rel_h": reversed_table(L0_conv_rel_pos_h), "rel_w": reversed_table(L0_conv_rel_pos_w),
    }
    nc = bacc.Bacc("TRN2", target_bir_lowering=False, num_devices=1)
    io = {name: nc.dram_tensor(f"in_{name}", a.shape, F32, kind="ExternalInput").ap() for name, a in arrays.items()}
    out = nc.dram_tensor("out", (TOK, C), F32, kind="ExternalOutput").ap()
    build(nc, io, out)
    r = run_bass_kernel_spmd(nc, [{f"in_{name}": a for name, a in arrays.items()}], core_ids=[0])
    return r.results[0]["out"].reshape(1, GRID, GRID, C)
```

```python
from contextlib import ExitStack

import concourse.bass as bass
from concourse import mybir

P = 128
GRID = 48
TOK = GRID * GRID
C = 768
NH = 12
HD = C // NH
F = 4 * C
KC = C // P
TT = TOK // P
CH = 384
NCH = TOK // CH
REL = 2 * GRID - 1
GW = 2 * REL
EPS = 1e-5
SCALE = float(HD) ** -0.5
LOWEST = -3.0e38
RING = 3
BH, BW = 8, 16

ALU = mybir.AluOpType
ACT = mybir.ActivationFunctionType
AX = mybir.AxisListType
F32 = mybir.dt.float32
F32R = mybir.dt.float32r
ds = bass.ds


def wait(eng, sem, value):
    if isinstance(value, int) and value <= 0:
        return
    eng.wait_ge(sem, value)


def passed(eng, count):
    eng.sem_inc(count, 1)


class Names:

    def __init__(self, nc, ctx):
        self.nc, self.ctx = nc, ctx

    def sb(self, name, shape, dt=F32):
        return self.ctx.enter_context(self.nc.sbuf_tensor(name, shape, dt))

    def ps(self, name, shape):
        return self.ctx.enter_context(self.nc.psum_tensor(name, shape, F32))

    def sem(self, name):
        return self.ctx.enter_context(self.nc.semaphore(name))


def statistics(v, x, stats, step):
    v.bn_stats(stats[:, 0:6], x[:, 0:CH]).then_inc(step, 1)
    v.bn_stats(stats[:, 6:12], x[:, CH:C]).then_inc(step, 1)


def inverse_variance(v, stats, mv, rvar, step, t):
    v.bn_aggr(mv[:, :], stats[:, :]).then_inc(step, 1)
    v.wait_ge(step, 5 * t + 3)
    v.tensor_scalar(rvar[:, :], mv[:, 1:2], EPS, None, ALU.add).then_inc(step, 1)
    v.wait_ge(step, 5 * t + 4)
    v.reciprocal(rvar[:, :], rvar[:, :]).then_inc(step, 1)


def normalise(v, out, x, mv, rstd):
    return v.tensor_scalar(out[:, :], x[:, :], mv[:, 0:1], rstd[:, 0:1], ALU.subtract, ALU.mult)


def phase_qkv(nc, io, con, scr, front):
    HALF = TT // 2
    GPIECES = (HALF + 1) // 2
    UNIT = KC * CH
    with ExitStack() as ctx:
        n = Names(nc, ctx)
        xT_hi, xT_lo = n.sb("xT_hi", [P, KC, TOK], F32R), n.sb("xT_lo", [P, KC, TOK], F32R)
        raw = n.sb("qkv_raw", [P, UNIT])
        w_hi, w_lo = front["keys"][:, 0:3 * UNIT], front["keys"][:, UNIT:4 * UNIT]
        yq = [n.sb(f"qk_y{i}", [P, CH]) for i in range(3)]
        slots = [n.sb(f"qkv_parts{i}", [P, 2 * CH], F32R) for i in range(3)]
        parts = [s[:, :].rearrange("p (a c) -> p a c", a=2) for s in slots]
        vparts = [s[:, :].rearrange("p (h a d) -> p h a d", a=2, d=HD) for s in slots]
        rel_hi, rel_lo = n.sb("rel_hi", [P, 2 * REL], F32R), n.sb("rel_lo", [P, 2 * REL], F32R)
        with ExitStack() as early:
            e = Names(nc, early)
            x = [e.sb(f"n1_x{i}", [P, C]) for i in range(3)]
            y = [e.sb(f"n1_y{i}", [P, KC, P]) for i in range(3)]
            stats = [e.sb(f"n1_stats{i}", [P, 12]) for i in range(3)]
            mv = [e.sb(f"n1_mv{i}", [P, 2]) for i in range(3)]
            rvar = [e.sb(f"n1_rvar{i}", [P, 1]) for i in range(3)]
            rstd = [e.sb(f"n1_rstd{i}", [P, 1]) for i in range(3)]
            table, warm = e.sb("n1_table", [P, 2 * REL]), e.sb("n1_warm", [P, 1])
        qst = [n.sb(f"rel_q{i}", [P, HALF * P], F32R) for i in range(2)]
        gs = [n.sb(f"rel_g{i}", [P, 4 + i, GW]) for i in range(2)]
        ps = [n.ps(f"qkv_ps{i}", [P, 512]) for i in range(3)]
        tp = [n.ps(f"n1_tp{i}", [P, 512]) for i in range(3)]
        gp = [n.ps(f"rel_ps{i}", [P, 512])[:, 0:2 * GW].rearrange("p (a c) -> p a c", a=2) for i in range(2)]
        x_in = [n.sem(f"n1_x_in{i}") for i in range(3)]
        gb_in, const_in, table_in = n.sem("n1_gb_in"), n.sem("n1_const_in"), n.sem("n1_table_in")
        rows_in, warmed = n.sem("n1_rows_in"), n.sem("n1_warmed")
        var_step, root, normed = n.sem("n1_var_step"), n.sem("n1_root"), n.sem("n1_normed")
        xT_done, y_done = n.sem("n1_xT_done"), n.sem("n1_y_done")
        x_hi, x_lo = n.sem("n1_x_hi"), n.sem("n1_x_lo")
        zeroed, sp_passed = n.sem("n1_zeroed"), n.sem("n1_sp_passed")
        tab_step, bias_done = n.sem("n1_tab_step"), n.sem("n1_bias_done")
        raw_in, w_hi_done, w_lo_done = n.sem("qkv_raw_in"), n.sem("qkv_w_hi_done"), n.sem("qkv_w_lo_done")
        mm, yq_done, hi_done, lo_done = (n.sem(f"qk_{s}") for s in ("mm", "y_done", "hi_done", "lo_done"))
        out = [n.sem(f"qk_out{i}") for i in range(3)]
        q_in = [n.sem(f"rel_q_in{i}") for i in range(2)]
        q_out = n.sem("rel_q_out")
        g_mm, g_ev = n.sem("rel_mm"), n.sem("rel_ev")
        g_out = [n.sem(f"rel_g_out{i}") for i in range(2)]
        v_mm, v_y, v_hi, v_lo = (n.sem(f"v_{s}") for s in ("mm", "y", "hi", "lo"))
        v_out = [n.sem(f"v_out{i}") for i in range(3)]

        def early_steps(eng, step, end=NCH):
            for r in range(3):
                for j in range(3):
                    step(r, j)
            with eng.Fori(3, end) as r:
                for j in range(3):
                    step(r, j)
            for r in range(end, NCH + 2):
                for j in range(3):
                    step(r, j)

        def tile(r, j, lag):
            t = 3 * r + j - lag
            return None if isinstance(t, int) and not 0 <= t < TT else t

        def product_of(r):
            return None if isinstance(r, int) and r < 2 else r - 2

        def qk_rounds(eng, u, body):
            with eng.Fori(0, NCH // 2) as i:
                for p in range(2):
                    body(u, 2 * i + p, p)

        def rel_pieces(body, j):
            for e in range(2 * j, min(2 * j + 2, GPIECES)):
                body(e, min(2, HALF - 2 * e))

        def rel_round(u, ch):
            return NCH * (u - 2) + ch

        with nc.Block() as block:

            @block.sync
            def _(sp):
                def load_x(t, j):
                    sp.dma_start(x[j][:, :], io["x"][ds(t * P, P), :]).then_inc(x_in[j], 16)

                def load_raw(u):
                    sp.wait_ge(w_lo_done, KC * u)
                    sp.dma_start(raw[:, :].rearrange("p (k c) -> p k c", c=CH),
                                 io["w_qkv"][:, :, u * CH:(u + 1) * CH]).then_inc(raw_in, 16)

                def store(u, ch, oc):
                    sp.wait_ge(lo_done, 18 * u + 3 * ch + oc + 1)
                    row = (3 * (u % 2) + oc) * P
                    dst = scr["qk"][u // 2, :, row:row + P, ds(ch * CH, CH)].rearrange("a p t -> p a t")
                    sp.dma_start(dst, parts[oc][:, :, :].bitcast(F32)).then_inc(out[oc], 16)

                def store_rel(r, s):
                    sp.wait_ge(g_ev, GPIECES * r + (GPIECES if s else 2) + 2)
                    dst = scr["g"][ds((r * HALF + 4 * s) * P, (4 + s) * P), :].rearrange("(a p) c -> p a c", p=P)
                    sp.dma_start(dst, gs[s][:, :, :]).then_inc(g_out[s], 16)

                def early(r, j):
                    t = tile(r, j, -1)
                    if t is not None and not (isinstance(t, int) and t < 3):
                        sp.wait_ge(xT_done, 2 * (t - 3) + 2)
                        passed(sp, sp_passed)
                        load_x(t, (j + 1) % 3)
                    ch = product_of(r)
                    if isinstance(r, int) and (r, j) == (NCH + 1, 0):
                        load_raw(2)
                    if ch is not None:
                        store(0, ch, j)
                    if isinstance(r, int) and r == 1 and j == 2:
                        load_raw(1)
                    if isinstance(r, int) and r == 2 and j == 2:
                        for dst, src in ((con["v_bias"], "v_b"), (con["proj_bias"], "proj_b"), (con["mlp_bias2"], "mlp_b2")):
                            sp.dma_start(dst[:, :], io[src].to_broadcast([P, C])).then_inc(rows_in, 16)

                load_x(0, 0)
                for dst, src in ((con["g1"], "ln1_g"), (con["b1n"], "ln1_b")):
                    sp.dma_start(dst[:, :], io[src]).then_inc(gb_in, 16)
                load_x(1, 1)
                sp.dma_start(raw[:, :].rearrange("p (k c) -> p k c", c=CH), io["w_qkv"][:, :, 0:CH]).then_inc(raw_in, 16)
                load_x(2, 2)
                for dst, src in ((con["g2"], "ln2_g"), (con["b2n"], "ln2_b"), (con["qk_b"], "qk_b"),
                                 (con["mlp_b1"], "mlp_b1")):
                    sp.dma_start(dst[:, :], io[src]).then_inc(const_in, 16)
                for half in range(2):
                    for j, src in enumerate(("rel_h", "rel_w")):
                        sp.dma_start(table[half * HD:(half + 1) * HD, j * REL:(j + 1) * REL],
                                     io[src]).then_inc(table_in, 16)
                early_steps(sp, early, NCH - 1)
                for s in range(2):
                    sp.sem_inc(g_out[s], 16)
                for s in range(3):
                    sp.sem_inc(v_out[s], 16)
                for u in range(1, 4):
                    if u < 3:
                        for s in range(3):
                            sp.wait_ge(out[s], 16 * NCH * u)
                        sp.sem_inc(q_out, 1)

                    def stores(u, ch, p):
                        for oc in range(3):
                            store(u, ch, oc)
                            if u > 1 and oc:
                                store_rel(rel_round(u, ch), oc - 1)

                    with sp.Fori(0, NCH // 2 - 1) as i:
                        for p in range(2):
                            stores(u, 2 * i + p, p)
                    stores(u, NCH - 2, 0)
                    load_raw(u + 2)
                    stores(u, NCH - 1, 1)
                for half in range(2):
                    for t in range(TT):
                        if half == 1 and t == 1:
                            sp.wait_ge(v_mm, TT)
                            for s in range(3):
                                sp.wait_ge(out[s], 16 * 24)
                            for s in range(2):
                                sp.wait_ge(g_out[s], 16 * 2 * 2 + 16)
                            load_queries(sp, scr, front, 0, 0)
                            load_terms(sp, scr, front, 0, 0)
                        if half == 1 and t in (3, 5, 7, 9):
                            load_first_keys(sp, scr, front, (t - 3) // 2)
                        if half == 1 and t == 11:
                            load_queries(sp, scr, front, 1, 0)
                            load_terms(sp, scr, front, 1, 0)
                        sp.wait_ge(v_lo, TT * half + t + 1)
                        dst = scr["v"][t * P:(t + 1) * P, half * (NH // 2):(half + 1) * (NH // 2), :, :]
                        sp.dma_start(dst, vparts[t % 3][:, :, :, :].bitcast(F32)).then_inc(v_out[t % 3], 16)
                        if t % 3:
                            store_rel(rel_round(4 + half, t // 3), t % 3 - 1)
                for s in range(3):
                    sp.wait_ge(v_out[s], 16 * 12 + 16)
                for s in range(2):
                    sp.wait_ge(g_out[s], 16 * 2 * NH + 16)

            @block.gpsimd
            def _(pool):
                pool.memset(con["ident"][:, :], 0.0).then_inc(zeroed, 1)
                pool.wait_ge(zeroed, 1)
                pool.affine_select(out=con["ident"][:, :], in_=con["ident"][:, :], compare_op=ALU.not_equal, fill=1.0,
                                   base=0, pattern=[[-1, P]], channel_multiplier=1).then_inc(con["ident_done"], 1)

                def early(r, j):
                    if isinstance(r, int) and 3 * r + j < KC:
                        piece = 3 * r + j
                        at = slice(piece * CH, (piece + 1) * CH)
                        pool.wait_ge(w_hi_done, piece + 1)
                        pool.tensor_tensor(w_lo[:, at], raw[:, at], w_hi[:, at].bitcast(F32),
                                           ALU.subtract).then_inc(w_lo_done, 1)
                    t = tile(r, j, 2)
                    if t is not None:
                        pool.wait_ge(x_hi, t + 1)
                        at = ds(t * P, P)
                        pool.tensor_tensor(xT_lo[:, :, at], y[(j - 2) % 3][:, :, :], xT_hi[:, :, at].bitcast(F32),
                                           ALU.subtract).then_inc(x_lo, 1)

                early_steps(pool, early)

                def load(i, p):
                    wait(pool, g_mm, GPIECES * (2 * i + p - 1))
                    for part in range(2):
                        pool.dma_start(qst[p][part * HD:(part + 1) * HD, :].bitcast(F32),
                                       scr["qk"][0, part, ds(i * HD, HD), p * HALF * P:(p + 1) * HALF * P])\
                            .then_inc(q_in[p], 16)

                pool.wait_ge(q_out, 1)
                for p in range(2):
                    load(0, p)
                with pool.Fori(1, NH // 2) as i:
                    for p in range(2):
                        load(i, p)
                pool.wait_ge(q_out, 2)
                with pool.Fori(NH // 2, NH) as i:
                    for p in range(2):
                        load(i, p)

            @block.tensor
            def _(pe):
                def turn(r, j):
                    t = tile(r, j, 1)
                    if t is None:
                        return
                    pe.wait_ge(normed, t + 1)
                    js = (j - 1) % 3
                    for b in range(2):
                        bank = (2 * js + b) % 3
                        wait(pe, y_done, 2 * t + b - 2)
                        for k in range(3):
                            last = pe.transpose(tp[bank][:, k * P:(k + 1) * P], x[js][:, (3 * b + k) * P:(3 * b + k + 1) * P],
                                                con["ident"][:, :])
                        last.then_inc(xT_done, 1)

                def product(u, ch, oc):
                    wait(pe, yq_done, 18 * u + 3 * ch + oc - 2)
                    for k in range(KC):
                        w0 = (u % 2) * 2 * UNIT + k * CH + oc * P
                        for q, (wt, xt) in enumerate(((w_hi, xT_hi), (w_hi, xT_lo), (w_lo, xT_hi))):
                            last = pe.matmul(ps[oc][:, 0:CH], wt[:, w0:w0 + P], xt[:, k, ds(ch * CH, CH)],
                                             start=(k == 0 and q == 0), stop=(k == KC - 1 and q == 2))
                    last.then_inc(mm, 1)

                def rel_products(r, p, j):
                    def piece(e, tiles):
                        if e == 0:
                            pe.wait_ge(q_in[p], 32 * (r // 2) + 32)
                        pe.wait_ge(g_ev, GPIECES * r + e + 1)
                        for a in range(tiles):
                            t = 2 * e + a
                            for q, tab in enumerate((rel_hi, rel_lo)):
                                last = pe.matmul(gp[(p + e) % 2][:, a, 0:2 * REL], qst[p][:, t * P:(t + 1) * P],
                                                 tab[:, :], start=(q == 0), stop=(q == 1))
                        last.then_inc(g_mm, 1)

                    rel_pieces(piece, j)

                def early(r, j):
                    ch = product_of(r)
                    if ch is not None:
                        if j == 0:
                            pe.wait_ge(x_lo, 3 * ch + 3)
                        product(0, ch, j)
                    turn(r, j)
                    if isinstance(r, int) and r == 1 and j == 2:
                        pe.wait_ge(w_lo_done, KC)

                pe.wait_ge(con["ident_done"], 1)
                early_steps(pe, early)
                pe.wait_ge(tab_step, 3)
                for u in range(1, 4):
                    pe.wait_ge(w_lo_done, KC * (u + 1))

                    def products(u, ch, p):
                        for oc in range(3):
                            product(u, ch, oc)
                            if u > 1:
                                rel_products(rel_round(u, ch), p, oc)

                    qk_rounds(pe, u, products)
                pe.wait_ge(w_lo_done, KC * 5)
                with pe.Fori(0, 2) as half:
                    for t in range(TT):
                        if t == 0:
                            pe.wait_ge(w_lo_done, KC * (5 + half))
                        pe.wait_ge(v_y, TT * half + t + 1)
                        for k in range(KC):
                            for q, (xt, wt) in enumerate(((xT_hi, w_hi), (xT_hi, w_lo), (xT_lo, w_hi))):
                                last = pe.matmul(ps[t % 3][:, 0:CH], xt[:, k, t * P:(t + 1) * P],
                                                 wt[:, ds(half * 2 * UNIT + k * CH, CH)],
                                                 start=(k == 0 and q == 0), stop=(k == KC - 1 and q == 2))
                        last.then_inc(v_mm, 1)
                        rel_products(rel_round(4 + half, t // 3), (t // 3) % 2, t % 3)

            @block.scalar
            def _(act):
                def high_piece(u, piece):
                    at = ds((u % 2) * 2 * UNIT + piece * CH, CH)
                    act.activation(w_hi[:, at], raw[:, ds(piece * CH, CH)], ACT.Copy).then_inc(w_hi_done, 1)

                def read_out(u, ch, oc):
                    t = 18 * u + 3 * ch + oc
                    act.wait_ge(mm, t + 1)
                    wait(act, lo_done, t - 2)
                    col = 3 * u + oc
                    if u < 2:
                        bias, scale = con["q_bias"][:, col:col + 1], SCALE
                    else:
                        bias, scale = con["qk_b"][:, col:col + 1], 1.0
                    act.activation(yq[oc][:, :], ps[oc][:, 0:CH], ACT.Identity, scale=scale,
                                   bias=bias).then_inc(yq_done, 1)

                def read_rel(r, p, j):
                    def piece(e, tiles):
                        act.wait_ge(g_mm, GPIECES * r + e + 1)
                        s = min(e // 2, 1)
                        if e in (0, 2):
                            act.wait_ge(g_out[s], 16 * r + 16)
                        act.activation(gs[s][:, 2 * e - 4 * s:2 * e - 4 * s + tiles, :], gp[(p + e) % 2][:, 0:tiles, :],
                                       ACT.Copy).then_inc(g_ev, 1)

                    rel_pieces(piece, j)

                def early(r, j):
                    t = tile(r, j, 0)
                    if t is not None:
                        act.wait_ge(var_step, 5 * t + 5)
                        act.activation(rstd[j][:, :], rvar[j][:, :], ACT.Sqrt).then_inc(root, 1)
                    if isinstance(r, int) and 3 * r + j < KC:
                        if 3 * r + j == 0:
                            act.wait_ge(raw_in, 16)
                        high_piece(0, 3 * r + j)
                    ch = product_of(r)
                    if ch is not None:
                        if j == 0:
                            if isinstance(r, int) and r == 2:
                                act.wait_ge(bias_done, 1)
                                act.wait_ge(raw_in, 32)
                            high_piece(1, ch)
                        read_out(0, ch, j)
                    t = tile(r, j, 1)
                    if t is not None:
                        js = (j - 1) % 3
                        wait(act, x_lo, t - 2)
                        for b in range(2):
                            act.wait_ge(xT_done, 2 * t + b + 1)
                            for k in range(3):
                                kc = 3 * b + k
                                last = act.activation(y[js][:, kc, :], tp[(2 * js + b) % 3][:, k * P:(k + 1) * P],
                                                      ACT.Identity, scale=con["g1"][:, kc:kc + 1],
                                                      bias=con["b1n"][:, kc:kc + 1])
                            last.then_inc(y_done, 1)

                act.wait_ge(con["ident_done"], 1)
                act.activation(warm[:, :], con["ident"][:, 0:1], ACT.Sqrt).then_inc(warmed, 1)
                act.wait_ge(gb_in, 32)
                early_steps(act, early)
                act.sem_inc(g_ev, 2)
                for u in range(1, 4):
                    act.wait_ge(mm, 18 * u)
                    act.wait_ge(raw_in, 16 * (u + 2))

                    def body(u, ch, p):
                        high_piece(u + 1, ch)
                        for oc in range(3):
                            read_out(u, ch, oc)
                            if u > 1:
                                read_rel(rel_round(u, ch), p, oc)

                    qk_rounds(act, u, body)
                act.wait_ge(mm, 18 * 4)
                act.wait_ge(raw_in, 16 * 6)
                act.activation(w_hi[:, 2 * UNIT:3 * UNIT], raw[:, :], ACT.Copy).then_inc(w_hi_done, KC)
                for s in range(3):
                    act.wait_ge(out[s], 16 * 24)
                with act.Fori(0, 2) as half:
                    for t in range(TT):
                        read_rel(rel_round(4 + half, t // 3), (t // 3) % 2, t % 3)
                        act.wait_ge(v_y, TT * half + t + 1 + RING)
                        act.wait_ge(v_out[t % 3], 16 * (6 * half + t // 3) + 16)
                        act.activation(vparts[t % 3][:, :, 0, :], yq[t % 3][:, :].rearrange("p (h d) -> p h d", d=HD),
                                       ACT.Copy).then_inc(v_hi, 1)

            @block.vector
            def _(v):
                def low_piece(u, piece):
                    v.wait_ge(w_hi_done, KC * u + piece + 1)
                    at = ds((u % 2) * 2 * UNIT + piece * CH, CH)
                    v.tensor_tensor(w_lo[:, at], raw[:, ds(piece * CH, CH)], w_hi[:, at].bitcast(F32),
                                    ALU.subtract).then_inc(w_lo_done, 1)

                def split(u, ch, oc):
                    t = 18 * u + 3 * ch + oc
                    v.wait_ge(yq_done, t + 1)
                    wait(v, out[oc], 16 * (6 * u + ch))
                    v.tensor_copy(parts[oc][:, 0, :], yq[oc][:, :]).then_inc(hi_done, 1)
                    v.wait_ge(hi_done, t + 1)
                    v.tensor_tensor(parts[oc][:, 1, :], yq[oc][:, :], parts[oc][:, 0, :].bitcast(F32),
                                    ALU.subtract).then_inc(lo_done, 1)

                def norm(t, j):
                    if t is None:
                        return
                    v.wait_ge(root, t + 1)
                    normalise(v, x[j], x[j], mv[j], rstd[j]).then_inc(normed, 1)

                def early(r, j):
                    t, before = tile(r, j, 0), tile(r, j, 1)
                    if t is not None:
                        v.wait_ge(x_in[j], 16 * (t // 3) + 16)
                        statistics(v, x[j], stats[j], var_step)
                        v.wait_ge(var_step, 5 * t + 2)
                    norm(before, (j - 1) % 3)
                    if t is not None:
                        inverse_variance(v, stats[j], mv[j], rvar[j], var_step, t)
                    t = tile(r, j, 2)
                    if t is not None:
                        v.wait_ge(y_done, 2 * t + 2)
                        v.tensor_copy(xT_hi[:, :, ds(t * P, P)], y[(j - 2) % 3][:, :, :]).then_inc(x_hi, 1)
                    ch = product_of(r)
                    if ch is not None:
                        if j == 0:
                            low_piece(1, ch)
                        split(0, ch, j)
                    if isinstance(r, int) and r == 1 and j == 2:
                        constants()

                def constants():
                    v.wait_ge(con["ident_done"], 1)
                    v.tensor_tensor(con["fold"][:, :], con["ident"][:, 0:HD], con["ident"][:, HD:P],
                                    ALU.add)
                    v.wait_ge(const_in, 16 * 4)
                    v.tensor_scalar(con["q_bias"][:, :], con["qk_b"][:, 0:KC], SCALE, None, ALU.mult).then_inc(bias_done, 1)
                    v.wait_ge(table_in, 64)
                    v.tensor_scalar(table[:, :], table[:, :], 1.0 / SCALE, None, ALU.mult).then_inc(tab_step, 1)
                    v.wait_ge(tab_step, 1)
                    v.tensor_copy(rel_hi[:, :], table[:, :]).then_inc(tab_step, 1)
                    v.wait_ge(tab_step, 2)
                    v.tensor_tensor(rel_lo[:, :], table[:, :], rel_hi[:, :].bitcast(F32),
                                    ALU.subtract).then_inc(tab_step, 1)

                early_steps(v, early)
                v.sem_inc(v_y, RING)
                for u in range(1, 4):
                    def body(u, ch, p):
                        low_piece(u + 1, ch)
                        for oc in range(3):
                            split(u, ch, oc)

                    qk_rounds(v, u, body)
                v.wait_ge(w_hi_done, KC * 6)
                v.tensor_tensor(w_lo[:, 2 * UNIT:3 * UNIT], raw[:, :], w_hi[:, 2 * UNIT:3 * UNIT].bitcast(F32),
                                ALU.subtract).then_inc(w_lo_done, KC)
                v.wait_ge(rows_in, 48)
                with v.Fori(0, 2) as half:
                    for t in range(TT):
                        n_tile = TT * half + t
                        v.wait_ge(v_mm, n_tile + 1)
                        v.tensor_tensor(yq[t % 3][:, :], ps[t % 3][:, 0:CH], con["v_bias"][:, ds(half * CH, CH)],
                                        ALU.add).then_inc(v_y, 1)
                        v.wait_ge(v_hi, n_tile + 1)
                        v.tensor_tensor(vparts[t % 3][:, :, 1, :], yq[t % 3][:, :].rearrange("p (h d) -> p h d", d=HD),
                                        vparts[t % 3][:, :, 0, :].bitcast(F32), ALU.subtract).then_inc(v_lo, 1)


def load_queries(sp, scr, front, gi, h):
    p = gi % 2
    for part in range(2):
        sp.dma_start(front["queries"][p][part * HD:(part + 1) * HD, :].bitcast(F32),
                     scr["qk"][0, part, ds(h * HD, HD), gi * CH:(gi + 1) * CH]).then_inc(front["q_in"][p], 16)


def load_terms(sp, scr, front, gi, h):
    p = gi % 2
    for a in range(3):
        base = (h * TOK + gi * CH + a * P) * GW
        rows = bass.AP(scr["g"].tensor, base + GRID - 1 - BH * gi, [[BW * GW - 1, BH], [GW, BW], [1, GRID]])
        cols = bass.AP(scr["g"].tensor, base + REL + GRID - 1 - BW * a, [[BW * GW, BH], [GW - 1, BW], [1, GRID]])
        for j, src in enumerate((rows, cols)):
            sp.dma_start(front["terms"][p][:, a, j * GRID:(j + 1) * GRID], src).then_inc(front["rel_in"][p], 16)


def load_first_keys(sp, scr, front, i):
    dup, part = i // 2, i % 2
    sp.dma_start(front["keys"][dup * HD:(dup + 1) * HD, part * TOK:(part + 1) * TOK].bitcast(F32),
                 scr["qk"][1, part, 0:HD, :]).then_inc(front["k_first"], 16)


def phase_attention(nc, io, con, scr, front, nxt):
    KEYS = 2 * CH
    GROUPS = NH * NCH
    LOOP_FROM = 4
    with ExitStack() as ctx:
        n_ = Names(nc, ctx)
        keys, qg, relg = front["keys"], front["queries"], front["terms"]
        values = n_.sb("values", [P, TT, 2 * HD], F32R)
        bias = nxt["o"] + [n_.sb("bias2", [P, KEYS])]
        probs = [n_.sb(f"probs{i}", [P, TOK]) for i in range(6)]
        pT_hi = [n_.sb(f"pT_hi{i}", [P, CH], F32R) for i in range(6)]
        pT_lo = [n_.sb(f"pT_lo{i}", [P, CH], F32R) for i in range(6)]
        mx = [n_.sb(f"max{i}", [P, 3]) for i in range(6)]
        nmax = [n_.sb(f"negmax{i}", [P, 1]) for i in range(6)]
        sums = [n_.sb(f"sums{i}", [P, 3, 3]) for i in range(2)]
        total = [n_.sb(f"total{i}", [P, 3]) for i in range(2)]
        rinv = [n_.sb(f"rinv{i}", [P, 3]) for i in range(2)]
        oT = [n_.sb(f"oT{i}", [P, CH]) for i in range(2)]
        o = [n_.sb(f"o{i}", [P, 3, HD]) for i in range(2)]
        w_raw = n_.sb("pr_w_raw", [P, KC * C])
        score_ps = [n_.ps(f"score_ps{i}", [P, 2, 512]) for i in range(2)]
        turn_ps = [n_.ps(f"turn_ps{i}", [P, 512]) for i in range(3)]
        out_ps = n_.ps("out_ps", [P, 512])

        q_in, rel_in = front["q_in"], front["rel_in"]
        k_in, sp_passed, v_passed = n_.sem("at_k_in"), n_.sem("at_sp_passed"), n_.sem("at_v_passed")
        v_in = [n_.sem(f"at_v_in{i}") for i in range(3)]
        scored, added, biased = n_.sem("at_scored"), n_.sem("at_added"), n_.sem("at_biased")
        maxed, exped = n_.sem("at_maxed"), n_.sem("at_exped")
        turned, hi_done, lo_done = n_.sem("at_turned"), n_.sem("at_hi_done"), n_.sem("at_lo_done")
        multiplied, oT_done, folded = n_.sem("at_multiplied"), n_.sem("at_oT_done"), n_.sem("at_folded")
        inverted, normed = n_.sem("at_inverted"), n_.sem("at_normed")
        o_out = [n_.sem(f"at_o_out{i}") for i in range(2)]

        def groups(eng, step):
            def group(g, p):
                for s in range(9):
                    step(g, p, s)

            for g in range(LOOP_FROM):
                group(g, g % 2)
            with eng.Fori(LOOP_FROM // 2, GROUPS // 2) as i:
                for p in range(2):
                    group(2 * i + p, p)
            for g in range(GROUPS, GROUPS + 2):
                group(g, g % 2)

        def earlier(g, p, s, lag):
            back = -((s - lag) // 9)
            g2 = g - back
            if isinstance(g2, int) and not 0 <= g2 < GROUPS:
                return None
            return g2, (p + back) % 2, (s - lag) % 9

        def none(g):
            return isinstance(g, int) and not 0 <= g < GROUPS

        with nc.Block() as block:

            @block.sync
            def _(sp):
                def load_group(g, gi, h):
                    if isinstance(g, int) and g >= GROUPS:
                        return
                    wait(sp, scored, 9 * (g - 1))
                    wait(sp, biased, 9 * (g - 1))
                    passed(sp, sp_passed)
                    load_queries(sp, scr, front, gi, h)
                    load_terms(sp, scr, front, gi, h)

                def load_keys(h):
                    wait(sp, scored, 9 * NCH * (h - 1))
                    passed(sp, sp_passed)
                    slot = (h % 2) * 2 * TOK
                    for dup in range(2):
                        for part in range(2):
                            sp.dma_start(keys[dup * HD:(dup + 1) * HD, ds(slot + part * TOK, TOK)].bitcast(F32),
                                         scr["qk"][1, part, ds(h * HD, HD), :]).then_inc(k_in, 16)

                def load_values(h, j):
                    wait(sp, multiplied, TT * (NCH * h - 1) + 6 * (j + 1) if not isinstance(h, int) or h else 0)
                    passed(sp, sp_passed)
                    src = scr["v"][j * 6 * P:(j + 1) * 6 * P, ds(h, 1), :, :].rearrange("(t p) h a d -> p (t h) (a d)", p=P)
                    sp.dma_start(values[:, j * 6:(j + 1) * 6, :].bitcast(F32), src).then_inc(v_in[j], 16)

                def store(g, gi, h):
                    if none(g):
                        return
                    sp.wait_ge(normed, g + 1)
                    passed(sp, sp_passed)
                    dst = scr["o"][gi * CH:(gi + 1) * CH, ds(h * HD, HD)].rearrange("(a p) c -> p a c", p=P)
                    sp.dma_start(dst, o[gi % 2][:, :, :]).then_inc(o_out[gi % 2], 16)

                def head(h, more=True):
                    for gi in range(NCH):
                        g = NCH * h + gi
                        if not (isinstance(g, int) and g == 0):
                            load_group(g + 1, (gi + 1) % NCH, h + (gi + 1) // NCH)
                        store(g - 2, (gi - 2) % NCH, h + (gi - 2) // NCH)
                        later = not (isinstance(h, int) and h == 0)
                        if gi == 0 and later:
                            load_values(h, 0)
                            load_values(h, 1)
                        if gi == 1 and later:
                            load_values(h, 2)
                        if gi == 1 and more:
                            load_keys(h + 1)

                for j in range(3):
                    load_values(0, j)
                sp.dma_start(w_raw[:, :], io["w_proj"].rearrange("p k c -> p (k c)"))\
                    .then_inc(nxt["w_in"], 16)
                head(0)
                with sp.Fori(1, NH - 1) as h:
                    head(h)
                head(NH - 1, more=False)
                for s in range(2):
                    sp.wait_ge(o_out[s], 16 * (GROUPS // 2 - 1))
                sp.wait_ge(added, 9 * GROUPS)
                for t in range(2):
                    sp.dma_start(nxt["o"][t][:, :], scr["o"][t * P:(t + 1) * P, :]).then_inc(nxt["o_in"][t], 16)
                store(GROUPS - 2, NCH - 2, NH - 1)
                store(GROUPS - 1, NCH - 1, NH - 1)
                for s in range(2):
                    sp.wait_ge(o_out[s], 16 * GROUPS // 2)

            @block.gpsimd
            def _(pool):
                def step(g, p, s):
                    if none(g):
                        return
                    n, qt, c = 9 * g + s, s // 3, s % 3
                    if s == 0:
                        pool.wait_ge(rel_in[p], 96 * (g // 2) + 96)
                    wait(pool, added, n - 2)
                    cols = relg[p][:, qt, GRID:2 * GRID].rearrange("p (a w) -> p a w", w=BW).unsqueeze(2)\
                        .to_broadcast([P, 3, BH, BW])
                    for half in range(2):
                        y0 = (2 * c + half) * BH
                        rows = relg[p][:, qt, y0:y0 + BH].unsqueeze(1).unsqueeze(3).to_broadcast([P, 3, BH, BW])
                        last = pool.tensor_tensor(
                            bias[c][:, half * CH:(half + 1) * CH].rearrange("p (a h w) -> p a h w", h=BH, w=BW),
                            rows, cols, ALU.add)
                    last.then_inc(biased, 1)

                groups(pool, step)

            @block.tensor
            def _(pe):
                def step(g, p, s):
                    n, qt, c = 9 * g + s, s // 3, s % 3
                    bank = score_ps[(p + s) % 2]
                    if s == 0 and not none(g):
                        pe.wait_ge(q_in[p], 32 * (g // 2) + 32)
                        wait(pe, k_in, 64 * (g // NCH))
                    if isinstance(g, int) and g == 0 and s == 0:
                        pe.wait_ge(front["k_first"], 64)
                    if not none(g):
                        wait(pe, added, n - 1)
                    if s == 6 and not none(g - 2):
                        pe.wait_ge(normed, g - 1)
                    if s == 4 and not none(g - 2):
                        pe.wait_ge(oT_done, g - 1)
                        if none(g):
                            wait(pe, added, 9 * GROUPS)
                        for t in range(3):
                            last = pe.matmul(bank[:, t // 2, CH + HD * (t % 2):CH + HD * (t % 2 + 1)],
                                             oT[p][:, t * P:(t + 1) * P], con["fold"][:, :], start=True, stop=True)
                        last.then_inc(folded, 1)
                    if not none(g):
                        slot = ((g // NCH) % 2) * 2 * TOK
                        for part in range(2):
                            for j in range(2):
                                last = pe.matmul(bank[:, j, 0:CH], qg[p][:, qt * P:(qt + 1) * P],
                                                 keys[:, ds(slot + (part * TOK + c * KEYS + j * CH), CH)],
                                                 start=(part == 0), stop=(part == 1))
                        last.then_inc(scored, 1)
                    turn = earlier(g, p, s, 11)
                    if turn:
                        g2, p2, u = turn
                        if u % 3 == 0:
                            pe.wait_ge(exped, 9 * g2 + 6 + u // 3 + 1)
                        for kt in (2 * u, 2 * u + 1):
                            wait(pe, lo_done, TT * g2 + kt - 2)
                            for t in range(3):
                                last = pe.transpose(turn_ps[kt % 3][:, t * P:(t + 1) * P],
                                                    probs[3 * p2 + t][:, kt * P:(kt + 1) * P], con["ident"][:, :])
                            last.then_inc(turned, 1)
                    product = earlier(g, p, s, 12)
                    if product:
                        g2, p2, u = product
                        if u % 3 == 0:
                            pe.wait_ge(v_in[u // 3], 16 * (g2 // NCH) + 16)
                        if u == 0:
                            wait(pe, oT_done, g2)
                        for kt in (2 * u, 2 * u + 1):
                            pe.wait_ge(lo_done, TT * g2 + kt + 1)
                            for q, part in enumerate((pT_hi, pT_lo)):
                                last = pe.matmul(out_ps[:, 0:CH], values[:, kt, :], part[kt % 6][:, :],
                                                 start=(kt == 0 and q == 0), stop=(kt == TT - 1 and q == 1))
                            last.then_inc(multiplied, 1)

                groups(pe, step)

            @block.vector
            def _(v):
                def score_waits(g, p, s):
                    if none(g):
                        return
                    n, c = 9 * g + s, s % 3
                    wait(v, turned, TT * (g - 2) + 6 * (c + 1) if not none(g - 2) else 0)
                    v.wait_ge(scored, n + 1)
                    v.wait_ge(biased, n + 1)
                    passed(v, v_passed)

                def step(g, p, s):
                    n, qt, c = 9 * g + s, s // 3, s % 3
                    bank = score_ps[(p + s) % 2]
                    tile = 3 * p + qt
                    score_waits(g, p, s)
                    if not none(g):
                        v.tensor_tensor_reduce(
                            out=probs[tile][:, c * KEYS:(c + 1) * KEYS].rearrange("p (a b) -> p a b", b=CH),
                            in0=bank[:, :, 0:CH], in1=bias[c][:, :].rearrange("p (a b) -> p a b", b=CH),
                            scale=1.0, scalar=LOWEST, op0=ALU.add, op1=ALU.max,
                            accum_out=mx[tile][:, c:c + 1]).then_inc(added, 1)
                    turn = earlier(g, p, s, 11)
                    if turn:
                        g2, p2, u = turn
                        for kt in (2 * u, 2 * u + 1):
                            v.wait_ge(hi_done, TT * g2 + kt + 1)
                            v.tensor_tensor(pT_lo[kt % 6][:, :], turn_ps[kt % 3][:, 0:CH],
                                            pT_hi[kt % 6][:, :].bitcast(F32), ALU.subtract).then_inc(lo_done, 1)
                    if c == 2 and not none(g):
                        v.wait_ge(added, n + 1)
                        v.tensor_reduce(nmax[tile][:, :], mx[tile][:, :], axis=AX.X, op=ALU.max,
                                        negate=True).then_inc(maxed, 1)
                    if s == 4 and not none(g - 2):
                        v.wait_ge(inverted, 2 * g - 2)
                        if not none(g - 4):
                            v.wait_ge(o_out[p], 16 * ((g - 2) // 2))
                        v.wait_ge(folded, g - 1)
                        v.tensor_tensor(o[p][:, 0:2, :], bank[:, 0, CH:512].rearrange("p (t d) -> p t d", d=HD),
                                        rinv[p][:, 0:2].unsqueeze(2).to_broadcast([P, 2, HD]), ALU.mult)
                        v.tensor_scalar(o[p][:, 2, :], bank[:, 1, CH:CH + HD], rinv[p][:, 2:3], None,
                                        ALU.mult).then_inc(normed, 1)
                    if s == 4 and not none(g - 1):
                        v.wait_ge(exped, 9 * g)
                        v.tensor_reduce(total[1 - p][:, :], sums[1 - p][:, :, :], axis=AX.X,
                                        op=ALU.add).then_inc(inverted, 1)
                    if s == 5 and not none(g - 1):
                        v.wait_ge(inverted, 2 * g - 1)
                        v.reciprocal(rinv[1 - p][:, :], total[1 - p][:, :]).then_inc(inverted, 1)
                    if isinstance(g, int) and g == GROUPS and s >= 3:
                        at = slice((s - 3) * C, (s - 2) * C)
                        v.wait_ge(nxt["w_split"], s - 2)
                        v.tensor_tensor(nxt["w_lo"][:, at], w_raw[:, at],
                                        nxt["w_hi"][:, at].bitcast(F32), ALU.subtract).then_inc(nxt["w_lo_done"], 1)

                groups(v, step)

            @block.scalar
            def _(act):
                def step(g, p, s):
                    turn = earlier(g, p, s, 11)
                    if turn:
                        g2, p2, u = turn
                        for kt in (2 * u, 2 * u + 1):
                            act.wait_ge(turned, TT * g2 + kt + 1)
                            wait(act, multiplied, TT * g2 + kt - 5)
                            act.activation(pT_hi[kt % 6][:, :], turn_ps[kt % 3][:, 0:CH], ACT.Copy).then_inc(hi_done, 1)
                    if s == 2 and not none(g - 2):
                        act.wait_ge(multiplied, TT * (g - 1))
                        wait(act, folded, g - 3)
                        act.activation(oT[p][:, :], out_ps[:, 0:CH], ACT.Copy).then_inc(oT_done, 1)
                    exp = earlier(g, p, s, 3)
                    if exp:
                        g2, p2, s2 = exp
                        qt, c = s2 // 3, s2 % 3
                        tile = 3 * p2 + qt
                        act.wait_ge(maxed, 3 * g2 + qt + 1)
                        at = probs[tile][:, c * KEYS:(c + 1) * KEYS]
                        act.activation(at, at, ACT.Exp, bias=nmax[tile][:, 0:1],
                                       accum_out=sums[p2][:, qt, c:c + 1]).then_inc(exped, 1)
                    if isinstance(g, int) and g == GROUPS and s >= 3:
                        act.wait_ge(nxt["w_in"], 16)
                        at = slice((s - 3) * C, (s - 2) * C)
                        act.activation(nxt["w_hi"][:, at], w_raw[:, at],
                                       ACT.Copy).then_inc(nxt["w_split"], 1)

                groups(act, step)


def phase_proj(nc, io, con, scr, nxt, mlp):
    with ExitStack() as ctx:
        n = Names(nc, ctx)
        w_hi, w_lo = nxt["w_hi"], nxt["w_lo"]
        o = nxt["o"]
        x = [n.sb(f"pr_x{i}", [P, C]) for i in range(2)]
        oT_hi = [n.sb(f"pr_oT_hi{i}", [P, KC * P], F32R) for i in range(2)]
        oT_lo = [n.sb(f"pr_oT_lo{i}", [P, KC * P], F32R) for i in range(2)]
        x2 = [n.sb(f"pr_x2{i}", [P, C]) for i in range(2)]
        acc = [n.sb(f"pr_acc{i}", [P, C]) for i in range(2)]
        xn = [n.sb(f"pr_xn{i}", [P, C]) for i in range(2)]
        y = [n.sb(f"pr_y{i}", [P, KC, P]) for i in range(2)]
        parts = [n.sb(f"pr_parts{i}", [P, 2, KC, P], F32R) for i in range(2)]
        stats = [n.sb(f"pr_stats{i}", [P, 12]) for i in range(2)]
        mv = [n.sb(f"pr_mv{i}", [P, 2]) for i in range(2)]
        rvar = [n.sb(f"pr_rvar{i}", [P, 1]) for i in range(2)]
        rstd = [n.sb(f"pr_rstd{i}", [P, 1]) for i in range(2)]
        o_ps = n.ps("pr_o_ps", [P, 2, 512])
        mm_ps = mlp["mm_ps"]
        x_ps = n.ps("pr_x_ps", [P, 2, 512])
        sp_passed = n.sem("pr_sp_passed")
        o_in = nxt["o_in"]
        x_in = [n.sem(f"pr_x_in{i}") for i in range(2)]
        oT_done, oT_hi_done, oT_lo_done = n.sem("pr_oT_done"), n.sem("pr_oT_hi_done"), n.sem("pr_oT_lo_done")
        xb_done, mm, x2_done, acc_done = n.sem("pr_xb_done"), n.sem("pr_mm"), n.sem("pr_x2_done"), n.sem("pr_acc_done")
        var_step, root, normed = n.sem("pr_var_step"), n.sem("pr_root"), n.sem("pr_normed")
        xT_done, y_done, split = n.sem("pr_xT_done"), n.sem("pr_y_done"), n.sem("pr_split")
        acc_out = [n.sem(f"pr_acc_out{i}") for i in range(2)]
        parts_out = [n.sem(f"pr_parts_out{i}") for i in range(2)]

        def tiles(eng, step, first=4, last=2):
            for t in range(first):
                step(t, t % 2)
            with eng.Fori(first // 2, (TT - last) // 2) as i:
                for p in range(2):
                    step(2 * i + p, p)
            for t in range(TT - last, TT):
                step(t, t % 2)

        with nc.Block() as block:

            @block.sync
            def _(sp):
                def load_o(t, p):
                    wait(sp, oT_done, t - 1)
                    passed(sp, sp_passed)
                    sp.dma_start(o[p][:, :], scr["o"][ds(t * P, P), :]).then_inc(o_in[p], 16)

                def load_x(t, p):
                    wait(sp, x2_done, t - 1)
                    passed(sp, sp_passed)
                    sp.dma_start(x[p][:, :], io["x"][ds(t * P, P), :]).then_inc(x_in[p], 16)

                def store(t, p):
                    sp.wait_ge(split, 2 * t + 2)
                    passed(sp, sp_passed)
                    sp.dma_start(scr["xT"][:, :, :, ds(t * P, P)], parts[p][:, :, :, :].bitcast(F32))\
                        .then_inc(parts_out[p], 16)

                def step(t, p):
                    more = not (isinstance(t, int) and t + 2 >= TT)
                    if not (isinstance(t, int) and t + 3 >= TT):
                        load_o(t + 3, 1 - p)
                    if not (isinstance(t, int) and t < 2):
                        store(t - 2, p)
                    if more:
                        load_x(t + 2, p)
                    if isinstance(t, int) and t in (5, 6, 8, 9):
                        tc, part = (t - 5) // 3, (t - 5) % 3
                        for s in range(2):
                            sp.wait_ge(parts_out[s], 16 * (2 + tc))
                        sp.dma_start(mlp["xT"][tc][:, part, :, :].bitcast(F32),
                                     scr["xT"][:, part, :, tc * CH:(tc + 1) * CH]).then_inc(mlp["first_x_in"][tc], 16)

                for t in range(2):
                    load_x(t, t)
                sp.dma_start(mlp["raw"][0][:, :].rearrange("p (k c) -> p k c", c=CH),
                             io["w_up"][:, :, 0:CH]).then_inc(mlp["raw_in"][0], 16)
                sp.dma_start(mlp["raw"][1][:, :].rearrange("p (f c) -> p f c", c=C),
                             io["w_down"][0:CH, :].rearrange("(f p) c -> p f c", p=P)).then_inc(mlp["raw_in"][1], 16)
                load_o(2, 0)
                tiles(sp, step, 10, 4)
                store(TT - 2, 0)
                store(TT - 1, 1)
                for s in range(2):
                    sp.wait_ge(parts_out[s], 16 * TT // 2)
                    sp.wait_ge(acc_out[s], 16 * TT // 2)

            @block.gpsimd
            def _(pool):
                def add_bias(t, p):
                    pool.wait_ge(x_in[p], 16 * (t // 2) + 16)
                    pool.tensor_tensor(x[p][:, :], x[p][:, :], con["proj_bias"][:, :], ALU.add).then_inc(xb_done, 1)

                def step(t, p):
                    if not (isinstance(t, int) and t + 1 >= TT):
                        add_bias(t + 1, 1 - p)
                    pool.wait_ge(x2_done, t + 1)
                    if not (isinstance(t, int) and t < 2):
                        pool.wait_ge(acc_out[p], 16 * (t // 2))
                    pool.tensor_tensor(acc[p][:, :], x2[p][:, :], con["mlp_bias2"][:, :], ALU.add).then_inc(acc_done, 1)
                    pool.wait_ge(acc_done, t + 1)
                    pool.dma_start(scr["acc"][ds(t * P, P), :], acc[p][:, :]).then_inc(acc_out[p], 16)
                    if isinstance(t, int) and 1 <= t <= 3:
                        at = slice((t - 1) * C, t * C)
                        for i in range(2):
                            pool.wait_ge(mlp["split_hi"][i], t)
                            pool.tensor_tensor(mlp["w_lo"][i][0][:, at], mlp["raw"][i][:, at],
                                               mlp["w_hi"][i][0][:, at].bitcast(F32), ALU.subtract)\
                                .then_inc(mlp["split_lo"][i], 1)

                add_bias(0, 0)
                tiles(pool, step)

            @block.tensor
            def _(pe):
                def turn_o(t, p):
                    pe.wait_ge(o_in[p], 16 * (t // 2) + 16)
                    wait(pe, oT_lo_done, t)
                    for k in range(KC):
                        last = pe.transpose(o_ps[:, k // 3, (k % 3) * P:(k % 3 + 1) * P],
                                            o[p][:, k * P:(k + 1) * P], con["ident"][:, :])
                    last.then_inc(oT_done, 1)

                def turn_x(t, p):
                    pe.wait_ge(normed, t + 1)
                    wait(pe, y_done, t)
                    for k in range(KC):
                        last = pe.transpose(x_ps[:, k // 3, (k % 3) * P:(k % 3 + 1) * P],
                                            xn[p][:, k * P:(k + 1) * P], con["ident"][:, :])
                    last.then_inc(xT_done, 1)

                def step(t, p):
                    if not (isinstance(t, int) and t + 1 >= TT):
                        turn_o(t + 1, 1 - p)
                    pe.wait_ge(oT_lo_done, t + 1)
                    wait(pe, x2_done, t)
                    for nh in range(2):
                        for k in range(KC):
                            at = slice(k * P, (k + 1) * P)
                            to = slice(k * C + nh * CH, k * C + (nh + 1) * CH)
                            for q, (a, w) in enumerate(((oT_hi, w_hi), (oT_hi, w_lo), (oT_lo, w_hi))):
                                last = pe.matmul(mm_ps[:, nh, 0:CH], a[p][:, at], w[:, to],
                                                 start=(k == 0 and q == 0), stop=(k == KC - 1 and q == 2))
                    last.then_inc(mm, 1)
                    if not (isinstance(t, int) and t == 0):
                        turn_x(t - 1, 1 - p)

                turn_o(0, 0)
                pe.wait_ge(nxt["w_lo_done"], KC)
                tiles(pe, step)
                pe.wait_ge(mlp["first_x_in"][0], 32)
                pe.wait_ge(mlp["split_lo"][0], 3)
                for f in range(3):
                    if f == 2:
                        turn_x(TT - 1, 1)
                        pe.wait_ge(x2_done, TT)
                    hidden_tile(pe, mlp["h_ps"][f], mlp["w_hi"][0][0], mlp["w_lo"][0][0], mlp["xT"][0], f)\
                        .then_inc(mlp["h_mm"], 1)

            @block.scalar
            def _(act):
                def high(t, p):
                    act.wait_ge(oT_done, t + 1)
                    wait(act, mm, t - 1)
                    act.activation(oT_hi[p][:, :].rearrange("p (a b) -> p a b", b=CH), o_ps[:, :, 0:CH],
                                   ACT.Copy).then_inc(oT_hi_done, 1)

                def scale_shift(t, p):
                    act.wait_ge(xT_done, t + 1)
                    wait(act, split, 2 * t - 2)
                    for k in range(KC):
                        last = act.activation(y[p][:, k, :], x_ps[:, k // 3, (k % 3) * P:(k % 3 + 1) * P],
                                              ACT.Identity, scale=con["g2"][:, k:k + 1], bias=con["b2n"][:, k:k + 1])
                    last.then_inc(y_done, 1)

                def step(t, p):
                    if not (isinstance(t, int) and t + 1 >= TT):
                        high(t + 1, 1 - p)
                    if not (isinstance(t, int) and t == 0):
                        scale_shift(t - 1, 1 - p)
                    act.wait_ge(var_step, 5 * t + 5)
                    act.activation(rstd[p][:, :], rvar[p][:, :], ACT.Sqrt).then_inc(root, 1)
                    if isinstance(t, int) and 1 <= t <= 3:
                        at = slice((t - 1) * C, t * C)
                        for i in range(2):
                            act.wait_ge(mlp["raw_in"][i], 16)
                            act.activation(mlp["w_hi"][i][0][:, at], mlp["raw"][i][:, at],
                                           ACT.Copy).then_inc(mlp["split_hi"][i], 1)

                high(0, 0)
                tiles(act, step)
                scale_shift(TT - 1, 1)

            @block.vector
            def _(v):
                def low(t, p):
                    v.wait_ge(oT_hi_done, t + 1)
                    v.tensor_tensor(oT_lo[p][:, :].rearrange("p (a b) -> p a b", b=CH), o_ps[:, :, 0:CH],
                                    oT_hi[p][:, :].bitcast(F32).rearrange("p (a b) -> p a b", b=CH),
                                    ALU.subtract).then_inc(oT_lo_done, 1)

                def split_tile(t, p):
                    v.wait_ge(y_done, t + 1)
                    if not (isinstance(t, int) and t < 2):
                        v.wait_ge(parts_out[p], 16 * (t // 2))
                    v.tensor_copy(parts[p][:, 0, :, :], y[p][:, :, :]).then_inc(split, 1)
                    v.wait_ge(split, 2 * t + 1)
                    v.tensor_tensor(parts[p][:, 1, :, :], y[p][:, :, :], parts[p][:, 0, :, :].bitcast(F32),
                                    ALU.subtract).then_inc(split, 1)

                def step(t, p):
                    if not (isinstance(t, int) and t + 1 >= TT):
                        low(t + 1, 1 - p)
                    v.wait_ge(mm, t + 1)
                    v.wait_ge(xb_done, t + 1)
                    wait(v, acc_done, t - 1)
                    v.tensor_tensor(x2[p][:, :].rearrange("p (a b) -> p a b", b=CH), mm_ps[:, :, 0:CH],
                                    x[p][:, :].rearrange("p (a b) -> p a b", b=CH), ALU.add).then_inc(x2_done, 1)
                    v.wait_ge(x2_done, t + 1)
                    statistics(v, x2[p], stats[p], var_step)
                    v.wait_ge(var_step, 5 * t + 2)
                    if not (isinstance(t, int) and t == 0):
                        split_tile(t - 1, 1 - p)
                    inverse_variance(v, stats[p], mv[p], rvar[p], var_step, t)
                    v.wait_ge(root, t + 1)
                    wait(v, xT_done, t - 1)
                    normalise(v, xn[p], x2[p], mv[p], rstd[p]).then_inc(normed, 1)

                low(0, 0)
                tiles(v, step)
                split_tile(TT - 1, 1)


def hidden_tile(pe, bank, w_hi, w_lo, xT, f):
    for k in range(KC):
        w0 = k * CH + f * P
        for q, (w, part) in enumerate(((w_hi, 0), (w_hi, 1), (w_lo, 0))):
            last = pe.matmul(bank[:, 0:CH], w[:, w0:w0 + P], xT[:, part, k, :],
                             start=(k == 0 and q == 0), stop=(k == KC - 1 and q == 2))
    return last


def phase_mlp(nc, io, con, scr, out, mlp):
    FG = F // CH
    UNITS = 2 * 3 * FG
    HT = TOK // 2
    with ExitStack() as ctx:
        n_ = Names(nc, ctx)

        def sem(name):
            return n_.sem(f"ml_{name}")

        xT = mlp["xT"] + [n_.sb("ml_xT2", [P, 2, KC, CH], F32R)]
        acc = n_.sb(f"ml_acc", [P, HT // P, C])
        raw = mlp["raw"]
        w_hi, w_lo = mlp["w_hi"], mlp["w_lo"]
        y = [mlp["rows"][i // 2][:, (i % 2) * CH:(i % 2 + 1) * CH] for i in range(3)]
        h_hi = [n_.sb(f"ml_h_hi{i}", [P, 3, CH], F32R) for i in range(2)]
        h_lo = [mlp["small"], n_.sb("ml_h_lo1", [P, 3, CH], F32R)]
        h_ps = mlp["h_ps"]
        o_ps = [mlp["mm_ps"][:, 1, :]] + [n_.ps(f"ml_o_ps{i}", [P, 512]) for i in (1, 2)]
        x_in = [sem(f"x_in{i}") for i in range(3)]
        acc_in, stored = [sem(f"acc_in{i}") for i in range(3)], [sem(f"stored{i}") for i in range(2)]
        raw_in, split_hi, split_lo = mlp["raw_in"], mlp["split_hi"], mlp["split_lo"]
        h_mm, gelu, hi_done, lo_done = mlp["h_mm"], sem("gelu"), sem("h_hi"), sem("h_lo")
        o_mm, added = sem("o_mm"), sem("added")
        b1 = [n_.sb(f"ml_b1_{i}", [P, 3]) for i in range(2)]
        b1_done = sem("b1_done")

        def units(eng, step):
            for m in range(6):
                step(m, m)
            with eng.Fori(1, UNITS // 6 - 1) as i:
                for j in range(6):
                    step(6 * i + j, j)
            for m in range(UNITS - 6, UNITS):
                step(m, m % 6)

        def group_of(m, j):
            return (m - j) // 3 + j // 3 if not isinstance(m, int) else m // 3

        def last_group(m):
            return isinstance(m, int) and m // 3 == 2 * FG - 1

        def rows(dram, hf, tc):
            at = hf * HT + tc * CH
            return dram[at:at + CH, :].rearrange("(t p) c -> p t c", p=P)

        with nc.Block() as block:

            @block.sync
            def _(sp):
                def load_raw(i, fg):
                    wait(sp, split_lo[i], 3 * fg)
                    if i == 0:
                        src = io["w_up"][:, :, ds((fg % FG) * CH, CH)]
                        dst = raw[0][:, :].rearrange("p (k c) -> p k c", c=CH)
                    else:
                        src = io["w_down"][ds((fg % FG) * CH, CH), :].rearrange("(f p) c -> p f c", p=P)
                        dst = raw[1][:, :].rearrange("p (f c) -> p f c", c=C)
                    sp.dma_start(dst, src).then_inc(raw_in[i], 16)

                def step(m, j):
                    if j % 3 and not (isinstance(m, int) and m // 3 >= 2 * FG - 2):
                        load_raw(j % 3 - 1, group_of(m, j) + 2)

                load_raw(0, 1)
                load_raw(1, 1)
                units(sp, step)
                for tc in range(3):
                    for tt in range(3):
                        sp.wait_ge(added, 6 * (UNITS - 3 + tc) + 2 * tt + 2)
                        at = HT + tc * CH + tt * P
                        sp.dma_start(out[at:at + P, :], acc[:, 3 * tc + tt, :]).then_inc(stored[1], 16)
                sp.wait_ge(stored[1], 16 * 9)

            @block.gpsimd
            def _(pool):
                def load_tokens(hf, tc):
                    at = hf * HT + tc * CH
                    for part in range(2):
                        pool.dma_start(xT[tc][:, part, :, :].bitcast(F32),
                                       scr["xT"][:, part, :, at:at + CH]).then_inc(x_in[tc], 16)

                def load_acc(hf, tc):
                    pool.dma_start(acc[:, 3 * tc:3 * tc + 3, :], rows(scr["acc"], hf, tc)).then_inc(acc_in[tc], 16)

                def copy_bias(fg):
                    wait(pool, gelu, 9 * (fg - 1))
                    at = 3 * (fg % FG)
                    pool.tensor_copy(b1[fg % 2][:, :], con["mlp_b1"][:, at:at + 3]).then_inc(b1_done, 1)

                copy_bias(0)
                load_acc(0, 0)
                load_tokens(0, 2)
                load_acc(0, 1)
                load_acc(0, 2)
                for fg in range(1, FG + 1):
                    copy_bias(fg)
                for tc in range(3):
                    m = 3 * (FG - 1) + tc
                    pool.wait_ge(h_mm, 3 * m + 3)
                    load_tokens(1, tc)
                    pool.wait_ge(added, 6 * m + 6)
                    pool.dma_start(rows(out, 0, tc), acc[:, 3 * tc:3 * tc + 3, :]).then_inc(stored[0], 16)
                    pool.wait_ge(stored[0], 16 * (tc + 1))
                    load_acc(1, tc)
                for fg in range(FG + 1, 2 * FG):
                    copy_bias(fg)

            @block.tensor
            def _(pe):
                def hidden(m, j):
                    tc, slot = j % 3, (j // 3) % 2
                    if tc == 0:
                        pe.wait_ge(split_lo[0], 3 * group_of(m, j) + 3)
                    wait(pe, x_in[tc], 32 * (m // (3 * FG)) + (32 if tc == 2 else 0))
                    if isinstance(m, int) and m == 1:
                        pe.wait_ge(mlp["first_x_in"][1], 32)
                    for f in range(3):
                        if isinstance(m, int) and m == 0:
                            continue
                        wait(pe, gelu, 3 * m + f - 2)
                        hidden_tile(pe, h_ps[f], w_hi[0][slot], w_lo[0][slot], xT[tc], f).then_inc(h_mm, 1)

                def down(m, j):
                    tc, slot = j % 3, (j // 3) % 2
                    if tc == 0:
                        pe.wait_ge(split_lo[1], 3 * group_of(m, j) + 3)
                    pe.wait_ge(lo_done, 3 * m + 3)
                    for r in range(6):
                        tt, nh = r // 2, r % 2
                        wait(pe, added, 6 * m + r - 2)
                        for f in range(3):
                            to = slice(f * C + nh * CH, f * C + (nh + 1) * CH)
                            for q, (h, w) in enumerate(((h_hi, w_hi), (h_hi, w_lo), (h_lo, w_hi))):
                                last = pe.matmul(o_ps[r % 3][:, 0:CH], h[j % 2][:, f, tt * P:(tt + 1) * P],
                                                 w[1][slot][:, to], start=(f == 0 and q == 0), stop=(f == 2 and q == 2))
                        last.then_inc(o_mm, 1)

                def step(m, j):
                    hidden(m, j)
                    if not (isinstance(m, int) and m == 0):
                        down(m - 1, (j - 1) % 6)

                units(pe, step)
                down(UNITS - 1, 5)

            @block.scalar
            def _(act):
                def split_piece(i, fg, slot, piece):
                    at = slice(piece * C, (piece + 1) * C)
                    act.activation(w_hi[i][slot][:, at], raw[i][:, at], ACT.Copy).then_inc(split_hi[i], 1)

                def step(m, j):
                    tc = j % 3
                    fg = group_of(m, j)
                    if tc and not last_group(m):
                        act.wait_ge(raw_in[tc - 1], 16 * (fg + 2))
                        wait(act, o_mm, 18 * fg)
                    if tc == 0:
                        act.wait_ge(b1_done, fg + 1)
                    for f in range(3):
                        if tc and not last_group(m):
                            split_piece(tc - 1, fg + 1, (j // 3 + 1) % 2, f)
                        n = 3 * m + f
                        wait(act, lo_done, n - 2)
                        act.wait_ge(h_mm, n + 1)
                        act.activation(y[f][:, :], h_ps[f][:, 0:CH], ACT.Gelu,
                                       bias=b1[(j // 3) % 2][:, f:f + 1]).then_inc(gelu, 1)

                units(act, step)

            @block.vector
            def _(v):
                def split_piece(i, fg, slot, piece):
                    at = slice(piece * C, (piece + 1) * C)
                    v.wait_ge(split_hi[i], 3 * fg + piece + 1)
                    v.tensor_tensor(w_lo[i][slot][:, at], raw[i][:, at], w_hi[i][slot][:, at].bitcast(F32),
                                    ALU.subtract).then_inc(split_lo[i], 1)

                def add_up(m, j):
                    tc = j % 3
                    v.wait_ge(acc_in[tc], 16 * (m // (3 * FG)) + 16)
                    for r in range(6):
                        tt, nh = r // 2, r % 2
                        q = 6 * m + r
                        v.wait_ge(o_mm, q + 1)
                        wait(v, added, q - 17)
                        at = acc[:, 3 * tc + tt, nh * CH:(nh + 1) * CH]
                        v.tensor_tensor(at, at, o_ps[r % 3][:, 0:CH], ALU.add).then_inc(added, 1)

                def step(m, j):
                    tc = j % 3
                    fg = group_of(m, j)
                    wait(v, o_mm, 6 * (m - 1))
                    for f in range(3):
                        if tc and not last_group(m):
                            split_piece(tc - 1, fg + 1, (j // 3 + 1) % 2, f)
                        n = 3 * m + f
                        v.wait_ge(gelu, n + 1)
                        v.tensor_copy(h_hi[j % 2][:, f, :], y[f][:, :]).then_inc(hi_done, 1)
                        v.wait_ge(hi_done, n + 1)
                        v.tensor_tensor(h_lo[j % 2][:, f, :], y[f][:, :], h_hi[j % 2][:, f, :].bitcast(F32),
                                        ALU.subtract).then_inc(lo_done, 1)
                    if not (isinstance(m, int) and m == 0):
                        add_up(m - 1, (j - 1) % 6)

                units(v, step)
                add_up(UNITS - 1, 5)


def build(nc, io, out):
    with ExitStack() as ctx:
        n = Names(nc, ctx)

        def dram(name, shape):
            return nc.dram_tensor(name, shape, F32, kind="Internal").ap()

        scr = {
            "qk": dram("qk_parts", (2, 2, C, TOK)),
            "v": dram("v_parts", (TOK, NH, 2, HD)),
            "g": dram("rel_products", (NH * TOK, GW)),
            "o": dram("attention_out", (TOK, C)),
            "acc": dram("x2_plus_b2", (TOK, C)),
            "xT": dram("norm2_parts", (P, 2, KC, TOK)),
        }
        con = {
            "ident": n.sb("ident", [P, P]), "fold": n.sb("fold", [P, HD]),
            "g1": n.sb("g1", [P, KC]), "b1n": n.sb("b1n", [P, KC]), "g2": n.sb("g2", [P, KC]), "b2n": n.sb("b2n", [P, KC]),
            "qk_b": n.sb("qk_b", [P, 2 * KC]), "q_bias": n.sb("q_bias", [P, KC]), "mlp_b1": n.sb("mlp_b1", [P, F // P]),
            "v_bias": n.sb("v_bias", [P, C]), "proj_bias": n.sb("proj_bias", [P, C]), "mlp_bias2": n.sb("mlp_bias2", [P, C]),
            "ident_done": n.sem("ident_done"),
        }
        keys, small = n.sb("keys", [P, 4 * TOK], F32R), n.sb("queries", [P, 3, CH], F32R)
        front = {
            "keys": keys, "queries": [small[:, i, :] for i in range(2)],
            "terms": [n.sb(f"rel{i}", [P, 3, 2 * GRID]) for i in range(2)],
            "q_in": [n.sem(f"at_q_in{i}") for i in range(2)], "rel_in": [n.sem(f"at_rel_in{i}") for i in range(2)],
            "k_first": n.sem("at_k_first"),
        }
        phase_qkv(nc, io, con, scr, front)
        with ExitStack() as rest:
            r = Names(nc, rest)
            mlp = {
                "first_x_in": [r.sem(f"ml_first_x_in{i}") for i in range(2)],
                "raw_in": [r.sem(f"ml_raw_in{i}") for i in range(2)],
                "split_hi": [r.sem(f"ml_split_hi{i}") for i in range(2)],
                "split_lo": [r.sem(f"ml_split_lo{i}") for i in range(2)],
            }
            proj = {
                "w_hi": r.sb("pr_w_hi", [P, KC * C], F32R), "w_lo": r.sb("pr_w_lo", [P, KC * C], F32R),
                "o": [r.sb(f"pr_o{i}", [P, C]) for i in range(2)], "o_in": [r.sem(f"pr_o_in{i}") for i in range(2)],
                "w_in": r.sem("pr_w_in"), "w_split": r.sem("pr_w_split"), "w_lo_done": r.sem("pr_w_lo_done"),
            }
            phase_attention(nc, io, con, scr, front, proj)
            mlp["rows"] = proj["o"]
            mlp["raw"] = [r.sb(f"ml_raw{i}", [P, KC * CH]) for i in range(2)]
            quarter = [slice(i * KC * CH, (i + 1) * KC * CH) for i in range(4)]
            mlp["w_hi"] = [[keys[:, quarter[i]], proj["w_hi"][:, quarter[i]]] for i in range(2)]
            mlp["w_lo"] = [[keys[:, quarter[2 + i]], proj["w_lo"][:, quarter[i]]] for i in range(2)]
            mlp["small"] = small
            mlp["xT"] = [r.sb(f"ml_xT{i}", [P, 2, KC, CH], F32R) for i in range(2)]
            mlp["mm_ps"] = r.ps("pr_mm_ps", [P, 2, 512])
            mlp["h_ps"] = [r.ps(f"ml_h_ps{i}", [P, 512]) for i in range(2)] + [mlp["mm_ps"][:, 0, :]]
            mlp["h_mm"] = r.sem("ml_h_mm")
            phase_proj(nc, io, con, scr, proj, mlp)
            phase_mlp(nc, io, con, scr, out, mlp)


def kernel(x, L0_conv_qkv_w, L0_conv_qkv_b, L0_conv_proj_w, L0_conv_proj_b, L0_conv_rel_pos_h, L0_conv_rel_pos_w,
           L0_conv_ln1_g, L0_conv_ln1_b, L0_conv_ln2_g, L0_conv_ln2_b, L0_conv_mlp_w1, L0_conv_mlp_b1,
           L0_conv_mlp_w2, L0_conv_mlp_b2):
    import numpy as np
    import concourse.bacc as bacc
    from concourse.bass_utils import run_bass_kernel_spmd

    def tiled(w):
        w = np.asarray(w)
        return np.ascontiguousarray(w.reshape(-1, P, w.shape[1]).transpose(1, 0, 2))

    def columns(b):
        return np.ascontiguousarray(np.asarray(b).reshape(-1, P).T)

    def reversed_table(r):
        return np.ascontiguousarray(np.asarray(r)[::-1].T)

    def blocked(tokens):
        return tokens.reshape(GRID // BH, BH, GRID // BW, BW, C).transpose(0, 2, 1, 3, 4).reshape(TOK, C)

    def unblocked(rows):
        return rows.reshape(GRID // BH, GRID // BW, BH, BW, C).transpose(0, 2, 1, 3, 4).reshape(1, GRID, GRID, C)

    qkv_b = np.asarray(L0_conv_qkv_b)
    arrays = {
        "x": np.ascontiguousarray(blocked(np.asarray(x))),
        "w_qkv": tiled(L0_conv_qkv_w), "w_proj": tiled(L0_conv_proj_w), "w_up": tiled(L0_conv_mlp_w1),
        "w_down": np.ascontiguousarray(L0_conv_mlp_w2),
        "qk_b": columns(qkv_b[:2 * C]), "v_b": qkv_b[None, 2 * C:].copy(),
        "proj_b": np.asarray(L0_conv_proj_b)[None, :].copy(), "mlp_b2": np.asarray(L0_conv_mlp_b2)[None, :].copy(),
        "mlp_b1": columns(L0_conv_mlp_b1),
        "ln1_g": columns(L0_conv_ln1_g), "ln1_b": columns(L0_conv_ln1_b),
        "ln2_g": columns(L0_conv_ln2_g), "ln2_b": columns(L0_conv_ln2_b),
        "rel_h": reversed_table(L0_conv_rel_pos_h), "rel_w": reversed_table(L0_conv_rel_pos_w),
    }
    nc = bacc.Bacc("TRN2", target_bir_lowering=False, num_devices=1)
    io = {name: nc.dram_tensor(f"in_{name}", a.shape, F32, kind="ExternalInput").ap() for name, a in arrays.items()}
    out = nc.dram_tensor("out", (TOK, C), F32, kind="ExternalOutput").ap()
    build(nc, io, out)
    r = run_bass_kernel_spmd(nc, [{f"in_{name}": a for name, a in arrays.items()}], core_ids=[0])
    return unblocked(r.results[0]["out"])
```
